# Optimizing a Trainium2 kernel written in Bass

```python
import numpy as np
import jax
import jax.numpy as jnp

def _softmax(x, axis=-1):
    return jax.nn.softmax(x, axis=axis)

def _gelu(x):
    return jax.nn.gelu(x, approximate=True)

def _silu(x):
    return jax.nn.silu(x)

def _sigmoid(x):
    return jax.nn.sigmoid(x)

def _layernorm(x, axis=-1, eps=1e-05):
    m = jnp.mean(x, axis=axis, keepdims=True)
    v = jnp.var(x, axis=axis, keepdims=True)
    return (x - m) / jnp.sqrt(v + eps)

def _scatter_add(tgt, idx, src, axis=0):
    return tgt.at[idx].add(src)

def _segment_sum(src, seg, n):
    return jax.ops.segment_sum(src, seg, n)
kernel_name = 'mk_prb_d2_jaxref_r8_e7b4b1'

def setup_inputs(seed: int=0):
    np.random.seed(seed)
    _w = jnp.asarray

    def _L0_attn_setup():
        import jax, jax.numpy as jnp
        import numpy as np
        GROUP = 64
        MAX_REL = 32

        def _silu(x):
            return x * jax.nn.sigmoid(x)

        def _ln(x, w, b, eps=1e-05):
            m = x.mean(-1, keepdims=True)
            v = ((x - m) ** 2).mean(-1, keepdims=True)
            return (x - m) / jnp.sqrt(v + eps) * w + b

        def _rope(x):
            n, d = (x.shape[-2], x.shape[-1])
            half = d // 2
            pos = jnp.arange(n, dtype=x.dtype)
            inv_freq = 10000.0 ** (-jnp.arange(half, dtype=x.dtype) / half)
            sinusoid = pos[:, None] * inv_freq[None, :]
            sin, cos = (jnp.sin(sinusoid), jnp.cos(sinusoid))
            x1, x2 = (x[..., :half], x[..., half:])
            return jnp.concatenate([x1 * cos - x2 * sin, x2 * cos + x1 * sin], axis=-1)
        key = jax.random.key(seed)
        ks = jax.random.split(key, 8)
        B, N, D, QK, H = (4, 512, 128, 32, 256)
        s = 0.02
        return {'x': jax.random.normal(ks[0], (B, N, D), dtype=jnp.float32), 'ln1_w': jnp.ones((D,), jnp.float32), 'ln1_b': jnp.zeros((D,), jnp.float32), 'Wqk': jax.random.normal(ks[1], (QK, D), jnp.float32) * s, 'bqk': jnp.zeros((QK,), jnp.float32), 'Wv': jax.random.normal(ks[2], (H, D), jnp.float32) * s, 'bv': jnp.zeros((H,), jnp.float32), 'Wg': jax.random.normal(ks[3], (H, D), jnp.float32) * s, 'bg': jnp.zeros((H,), jnp.float32), 'Wo': jax.random.normal(ks[4], (D, H), jnp.float32) * s, 'bo': jnp.zeros((D,), jnp.float32), 'ln2_w': jnp.ones((D,), jnp.float32), 'ln2_b': jnp.zeros((D,), jnp.float32), 'gamma': jax.random.normal(ks[5], (4, QK), jnp.float32) * 0.02, 'beta': jnp.zeros((4, QK), jnp.float32), 'pos_emb': jax.random.normal(ks[6], (2 * MAX_REL + 1,), jnp.float32)}
    _L0_attn_in = _L0_attn_setup()

    def _L0_ffn_setup():
        import jax, jax.numpy as jnp
        import numpy as np
        TOP_K = 8
        key = jax.random.key(seed)
        ks = jax.random.split(key, 6)
        B, S, D, F, E = (2, 128, 128, 64, 64)
        x = jax.random.normal(ks[0], (B, S, D), dtype=jnp.float32)
        centroids = jax.random.normal(ks[1], (E, D), dtype=jnp.float32) * 0.05
        expert_biases = jnp.zeros((E,), dtype=jnp.float32)
        Ws_up = jax.random.normal(ks[2], (D, F), dtype=jnp.float32) / np.sqrt(D)
        Ws_down = jax.random.normal(ks[3], (F, D), dtype=jnp.float32) / np.sqrt(F)
        W_up = jax.random.normal(ks[4], (E, D, F), dtype=jnp.float32) / np.sqrt(D)
        W_down = jax.random.normal(ks[5], (E, F, D), dtype=jnp.float32) / np.sqrt(F)
        return {'x': x, 'centroids': centroids, 'expert_biases': expert_biases, 'Ws_up': Ws_up, 'Ws_down': Ws_down, 'W_up': W_up, 'W_down': W_down}
    _L0_ffn_in = _L0_ffn_setup()

    def _L1_attn_setup():
        import jax, jax.numpy as jnp
        import numpy as np
        import math
        B, S, D, H = (4, 256, 128, 16)
        DK = D // H
        key = jax.random.key(seed)
        ks = jax.random.split(key, 5)
        scale = 1.0 / math.sqrt(D)
        return {'x': jax.random.normal(ks[0], (B, S, D), dtype=jnp.float32), 'Wv': jax.random.normal(ks[1], (D, D), dtype=jnp.float32) * scale, 'bv': jax.random.normal(ks[2], (D,), dtype=jnp.float32) * scale, 'Wo': jax.random.normal(ks[3], (D, D), dtype=jnp.float32) * scale, 'bo': jax.random.normal(ks[4], (D,), dtype=jnp.float32) * scale}
    _L1_attn_in = _L1_attn_setup()

    def _L1_ffn_setup():
        import jax, jax.numpy as jnp
        import numpy as np
        E, TOP_K, D, H = (8, 2, 128, 256)
        B, S = (2, 256)
        key = jax.random.key(seed)
        ks = jax.random.split(key, 10)
        s = 0.02
        return {'x': jax.random.normal(ks[0], (B, S, D), dtype=jnp.float32), 'gate_w': jax.random.normal(ks[1], (E, D), dtype=jnp.float32) * s, 'gate_b': jnp.zeros((E,), dtype=jnp.float32), 'w0': jax.random.normal(ks[2], (E, H, D), dtype=jnp.float32) * s, 'b0': jnp.zeros((E, H), dtype=jnp.float32), 'w1': jax.random.normal(ks[3], (E, H, D), dtype=jnp.float32) * s, 'b1': jnp.zeros((E, H), dtype=jnp.float32), 'w2': jax.random.normal(ks[4], (E, D, H), dtype=jnp.float32) * s, 'b2': jnp.zeros((E, D), dtype=jnp.float32)}
    _L1_ffn_in = _L1_ffn_setup()
    _d = {'L0_attn_x': _L0_attn_in['x'], 'L0_attn_ln1_w': _L0_attn_in['ln1_w'], 'L0_attn_ln1_b': _L0_attn_in['ln1_b'], 'L0_attn_Wqk': _L0_attn_in['Wqk'], 'L0_attn_bqk': _L0_attn_in['bqk'], 'L0_attn_Wv': _L0_attn_in['Wv'], 'L0_attn_bv': _L0_attn_in['bv'], 'L0_attn_Wg': _L0_attn_in['Wg'], 'L0_attn_bg': _L0_attn_in['bg'], 'L0_attn_Wo': _L0_attn_in['Wo'], 'L0_attn_bo': _L0_attn_in['bo'], 'L0_attn_ln2_w': _L0_attn_in['ln2_w'], 'L0_attn_ln2_b': _L0_attn_in['ln2_b'], 'L0_attn_gamma': _L0_attn_in['gamma'], 'L0_attn_beta': _L0_attn_in['beta'], 'L0_attn_pos_emb': _L0_attn_in['pos_emb'], 'L0_ffn_centroids': _L0_ffn_in['centroids'], 'L0_ffn_expert_biases': _L0_ffn_in['expert_biases'], 'L0_ffn_Ws_up': _L0_ffn_in['Ws_up'], 'L0_ffn_Ws_down': _L0_ffn_in['Ws_down'], 'L0_ffn_W_up': _L0_ffn_in['W_up'], 'L0_ffn_W_down': _L0_ffn_in['W_down'], 'L1_attn_Wv': _L1_attn_in['Wv'], 'L1_attn_bv': _L1_attn_in['bv'], 'L1_attn_Wo': _L1_attn_in['Wo'], 'L1_attn_bo': _L1_attn_in['bo'], 'L1_ffn_gate_w': _L1_ffn_in['gate_w'], 'L1_ffn_gate_b': _L1_ffn_in['gate_b'], 'L1_ffn_w0': _L1_ffn_in['w0'], 'L1_ffn_b0': _L1_ffn_in['b0'], 'L1_ffn_w1': _L1_ffn_in['w1'], 'L1_ffn_b1': _L1_ffn_in['b1'], 'L1_ffn_w2': _L1_ffn_in['w2'], 'L1_ffn_b2': _L1_ffn_in['b2']}
    _x0 = _d['L0_attn_x']
    _d['L0_attn_x'] = jax.random.normal(jax.random.fold_in(jax.random.key(seed), 1), (4, 1024, 128), dtype=_x0.dtype)
    del _x0
    return _d

def reference(L0_attn_x, L0_attn_ln1_w, L0_attn_ln1_b, L0_attn_Wqk, L0_attn_bqk, L0_attn_Wv, L0_attn_bv, L0_attn_Wg, L0_attn_bg, L0_attn_Wo, L0_attn_bo, L0_attn_ln2_w, L0_attn_ln2_b, L0_attn_gamma, L0_attn_beta, L0_attn_pos_emb, L0_ffn_centroids, L0_ffn_expert_biases, L0_ffn_Ws_up, L0_ffn_Ws_down, L0_ffn_W_up, L0_ffn_W_down, L1_attn_Wv, L1_attn_bv, L1_attn_Wo, L1_attn_bo, L1_ffn_gate_w, L1_ffn_gate_b, L1_ffn_w0, L1_ffn_b0, L1_ffn_w1, L1_ffn_b1, L1_ffn_w2, L1_ffn_b2):

    def _L0_attn_ref(x, ln1_w, ln1_b, Wqk, bqk, Wv, bv, Wg, bg, Wo, bo, ln2_w, ln2_b, gamma, beta, pos_emb):
        import jax, jax.numpy as jnp
        import numpy as np
        GROUP = 64
        MAX_REL = 32

        def _silu(x):
            return x * jax.nn.sigmoid(x)

        def _ln(x, w, b, eps=1e-05):
            m = x.mean(-1, keepdims=True)
            v = ((x - m) ** 2).mean(-1, keepdims=True)
            return (x - m) / jnp.sqrt(v + eps) * w + b

        def _rope(x):
            n, d = (x.shape[-2], x.shape[-1])
            half = d // 2
            pos = jnp.arange(n, dtype=x.dtype)
            inv_freq = 10000.0 ** (-jnp.arange(half, dtype=x.dtype) / half)
            sinusoid = pos[:, None] * inv_freq[None, :]
            sin, cos = (jnp.sin(sinusoid), jnp.cos(sinusoid))
            x1, x2 = (x[..., :half], x[..., half:])
            return jnp.concatenate([x1 * cos - x2 * sin, x2 * cos + x1 * sin], axis=-1)
        b, n, d = x.shape
        G = GROUP
        x = _ln(x, ln1_w, ln1_b)
        qk = _silu(x @ Wqk.T + bqk)
        v = _silu(x @ Wv.T + bv)
        heads = qk[..., None, :] * gamma + beta
        quad_q, lin_q, quad_k, lin_k = (heads[..., i, :] for i in range(4))
        quad_q, lin_q, quad_k, lin_k = map(_rope, (quad_q, lin_q, quad_k, lin_k))
        g = n // G
        rs = lambda t: t.reshape(b, g, G, t.shape[-1])
        qq, lq, qkk, lk, vg = map(rs, (quad_q, lin_q, quad_k, lin_k, v))
        idx = jnp.arange(G)
        dist = jnp.clip(jnp.abs(idx[:, None] - idx[None, :]), 0, MAX_REL)
        bias = pos_emb[dist]
        quad_att = jnp.einsum('bgid,bgjd->bgij', qq, qkk) / G + bias
        attn = jax.nn.relu(quad_att) ** 2
        quad_out = jnp.einsum('bgij,bgje->bgie', attn, vg)
        lin_kv = jnp.einsum('bgnd,bgne->bde', lk, vg) / n
        lin_out = jnp.einsum('bgnd,bde->bgne', lq, lin_kv)
        qo = quad_out.reshape(b, n, -1)
        lo = lin_out.reshape(b, n, -1)
        gate = _silu(x @ Wg.T + bg)
        out = gate * (qo + lo)
        out = out @ Wo.T + bo
        return _ln(out, ln2_w, ln2_b)

    def _L0_ffn_ref(x, centroids, expert_biases, Ws_up, Ws_down, W_up, W_down):
        import jax, jax.numpy as jnp
        import numpy as np
        TOP_K = 8
        B, S, D = x.shape
        E = centroids.shape[0]
        T = B * S
        xf = x.reshape(T, D)
        shared = jax.nn.silu(xf @ Ws_up) @ Ws_down
        aff = xf @ centroids.T
        biased = aff + expert_biases
        _, idx = jax.lax.top_k(biased, TOP_K)
        sel = jnp.take_along_axis(aff, idx, axis=1)
        w = jax.nn.sigmoid(sel)
        w = w / (jnp.sum(w, axis=-1, keepdims=True) + 1e-08)
        cw = jnp.zeros((T, E), dtype=x.dtype).at[jnp.arange(T)[:, None], idx].add(w)
        h = jax.nn.silu(jnp.einsum('td,edf->etf', xf, W_up))
        y = jnp.einsum('etf,efd->etd', h, W_down)
        routed = jnp.einsum('etd,te->td', y, cw)
        return (shared + routed).reshape(B, S, D)

    def _L1_attn_ref(x, Wv, bv, Wo, bo):
        import jax, jax.numpy as jnp
        import numpy as np
        import math
        B, S, D, H = (4, 256, 128, 16)
        DK = D // H
        b, s, d = x.shape
        h, dk = (H, DK)
        p = jnp.einsum('bsd,ed->bse', x, Wv) + bv
        p = p.reshape(b, s, h, dk).transpose(0, 2, 1, 3)
        q = k = v = p
        scores = jnp.einsum('bhqd,bhkd->bhqk', q, k) / math.sqrt(dk)
        attn = jax.nn.softmax(scores, axis=-1)
        out = jnp.einsum('bhqk,bhkd->bhqd', attn, v)
        out = out.reshape(b, s, h * dk)
        return jnp.einsum('bsd,ed->bse', out, Wo) + bo

    def _L1_ffn_ref(x, gate_w, gate_b, w0, b0, w1, b1, w2, b2):
        import jax, jax.numpy as jnp
        import numpy as np
        E, TOP_K, D, H = (8, 2, 128, 256)
        B, S = (2, 256)
        Bn, Sq, Dv = x.shape
        xt = x.reshape(-1, Dv)
        logits = xt @ gate_w.T + gate_b
        top_v, top_i = jax.lax.top_k(logits, TOP_K)
        h0 = jnp.einsum('td,ehd->eth', xt, w0) + b0[:, None, :]
        h1 = jnp.einsum('td,ehd->eth', xt, w1) + b1[:, None, :]
        act = h0 * jax.nn.silu(h1)
        out_all = jnp.einsum('eth,edh->etd', act, w2) + b2[:, None, :]
        out_te = jnp.transpose(out_all, (1, 0, 2))
        sel = jnp.take_along_axis(out_te, top_i[:, :, None], axis=1)
        w = jax.nn.softmax(top_v, axis=-1)[:, :, None]
        out = (w * sel).sum(axis=1)
        return out.reshape(Bn, Sq, Dv)
    x = L0_attn_x
    xn = _layernorm(x, axis=-1)
    x = x + _L0_attn_ref(xn, L0_attn_ln1_w, L0_attn_ln1_b, L0_attn_Wqk, L0_attn_bqk, L0_attn_Wv, L0_attn_bv, L0_attn_Wg, L0_attn_bg, L0_attn_Wo, L0_attn_bo, L0_attn_ln2_w, L0_attn_ln2_b, L0_attn_gamma, L0_attn_beta, L0_attn_pos_emb) + _L0_ffn_ref(xn, L0_ffn_centroids, L0_ffn_expert_biases, L0_ffn_Ws_up, L0_ffn_Ws_down, L0_ffn_W_up, L0_ffn_W_down)
    xn = _layernorm(x, axis=-1)
    x = x + _L1_attn_ref(xn, L1_attn_Wv, L1_attn_bv, L1_attn_Wo, L1_attn_bo) + _L1_ffn_ref(xn, L1_ffn_gate_w, L1_ffn_gate_b, L1_ffn_w0, L1_ffn_b0, L1_ffn_w1, L1_ffn_b1, L1_ffn_w2, L1_ffn_b2)
    return x

_drawn_inputs = setup_inputs


def setup_inputs(seed=0):
    import zlib

    import numpy as np

    out = dict(_drawn_inputs(seed))
    spreads = {'L0_attn_ln1_w': (1.0, 0.2),
     'L0_attn_ln1_b': (0.0, 0.1),
     'L0_attn_bqk': (0.0, 0.8),
     'L0_attn_bv': (0.0, 0.1),
     'L0_attn_bg': (0.0, 0.1),
     'L0_attn_bo': (0.0, 0.1),
     'L0_attn_ln2_w': (1.0, 0.2),
     'L0_attn_ln2_b': (0.0, 0.1),
     'L0_attn_beta': (0.0, 0.8),
     'L0_ffn_expert_biases': (0.0, 0.1),
     'L1_ffn_gate_b': (0.0, 0.338),
     'L1_ffn_b0': (0.0, 0.8),
     'L1_ffn_b1': (0.0, 0.8),
     'L1_ffn_b2': (0.0, 0.549)}
    factors = {'L0_attn_Wqk': 8.0,
     'L0_attn_gamma': 8.0,
     'L1_ffn_w0': 8.0,
     'L1_ffn_w1': 8.0,
     'L1_ffn_w2': 8.0,
     'L1_attn_bo': 3.117}
    for name, (base, spread) in spreads.items():
        noise = np.random.default_rng([zlib.crc32(name.encode()), seed]).standard_normal(out[name].shape)
        drawn = base * np.exp(spread * noise) if base else spread * noise
        out[name] = jnp.asarray(drawn.astype(out[name].dtype))
    for name, factor in factors.items():
        out[name] = (out[name] * factor).astype(out[name].dtype)
    return out
```

```python
from contextlib import ExitStack

import numpy as np

import concourse.bass as bass
from concourse import mybir

ALU = mybir.AluOpType
ACT = mybir.ActivationFunctionType
AX = mybir.AxisListType
F32 = mybir.dt.float32
R32 = mybir.dt.float32r

P = 128
EPS = 1e-5
LOWEST = -3.0e38
CREDIT = 4


def shape_constants(N, QK, GROUP, MAX_REL):
    half = QK // 2
    pos = np.arange(N, dtype=np.float32)
    inv = (np.float32(10000.0) ** (-np.arange(half, dtype=np.float32) / np.float32(half))).astype(np.float32)
    ang = (pos[:, None] * inv[None, :]).astype(np.float32)
    sin, cos = np.sin(ang).astype(np.float32), np.cos(ang).astype(np.float32)
    heads = P // QK
    cos_t = np.tile(np.concatenate([cos, cos], 1).T, (heads, 1))
    sin_t = np.tile(np.concatenate([-sin, sin], 1).T, (heads, 1))
    dist = np.clip(np.abs(np.arange(GROUP)[:, None] - np.arange(GROUP)[None, :]), 0, MAX_REL)
    onehot = (dist[:, :, None] == np.arange(MAX_REL + 1)).astype(np.float32)
    k = np.arange(P)
    return {
        "c_cos": cos_t.astype(np.float32),
        "c_sin": sin_t.astype(np.float32),
        "c_dist": np.concatenate([onehot, onehot], 0).reshape(P, -1),
        "c_ident": np.eye(P, dtype=np.float32),
        "c_pick64": (k[:, None] % 64 == np.arange(64)[None, :]).astype(np.float32),
        "c_pick8": (np.arange(16)[:, None] % 8 == np.arange(8)[None, :]).astype(np.float32),
    }


def build_program(nc, a, out):
    B, N, D = a["x"].shape
    T = B * N
    SUB = T // P
    SB = N // P
    TB = 512
    NT = T // TB
    GROUP = 64
    NREL = a["pos_emb"].shape[1]
    E0 = a["centroids"].shape[1]
    PAIRS = E0 // 2
    UN0 = PAIRS + 1
    E1 = a["gate_w"].shape[1]
    HV = a["bv0"].shape[1]
    H1 = HV // P
    U1 = 2 * E1
    HG = 4
    DK = 8
    NG = B * HG
    LAG = 3
    WCH = 4
    MAXIMA = 2 * 4 * HG * (N // TB)
    CARRY = 16
    SLOTS, T1, T0 = MAXIMA + 2, CARRY + 3, CARRY + 35
    PRO, PRO_T0 = MAXIMA - CARRY + 1, 38
    SLOTS_END = CARRY + 1
    OD_W = ("od_even", "od_odd")
    MR = 3 * HG * DK
    AV0 = 17
    NI = N // 16
    SCALE = 1.0 / float(DK) ** 0.5

    ctx = ExitStack()
    with ctx:
        names = """
        passed pickw od_even od_odd ot_in xfp w_in c_in x_in qqd ph_w lr m_w m_r out_s w2_in peb_m bias_q wz_h wz_l x_var x_std xn z_var
        z_std z xt xf xth xtl zt zf zth ztl aff sig bi cs cst cwt qp qs qa qb qr v1p v2p vb1 vb2 v1
        v2 g0p g1p g0 g1 lkt lk kvp kv st tb att ot0 ot1 og0 og1 yp y y_var y_std yn yw yb xr wu_h
        wu_l wd_h wd_l up bc silu hf hi lo down yt ytp d_x e_var e_std exn ext exf exth extl lg
        shift ex gs gt pp pf ph pl vp ve va sc exq av osb mx red neg mhi l_zero gss gstp pj w1_h
        w1_l w2_h w2_l b2_h b2_l h1 h0 bg s1 ah hf1 hi1 lo1 dn1 rec on y2s ytp2 fin route rope
        route2 x_own z_own y_own e_own
        """.split()
        sem = {n: ctx.enter_context(nc.semaphore("s_" + n)) for n in names}

        base = (nc.sbuf_base + 63) // 64 * 64
        KB = 1024
        place = {}

        def region(name, start, size):
            place[name] = [base + start, base + start + size]

        def sb(where, name, shape, dt=F32):
            at, end = place[where]
            size = 4 * int(np.prod(shape[1:]))
            size = (size + 31) // 32 * 32
            assert at + size <= end, (where, name, at + size - end)
            place[where][0] = at + size
            return nc.alloc_sbuf_tensor_at(name, shape, dt, offset=at)

        region("keep", 0, 54 * KB)
        region("ffn0_lo", 54 * KB, 33 * KB)
        region("ffn0_hi", 87 * KB, 33 * KB)
        region("gates", 120 * KB, 16 * KB)
        region("work", 136 * KB, 71 * KB + 512)
        region("attn0", 87 * KB, 33 * KB)
        region("attn0w", 120 * KB + 16 * KB, 71 * KB + 512)
        region("attn1b", 54 * KB, 64 * KB)
        region("v_all", 120 * KB, 16 * KB)
        region("ffn1_lo", 136 * KB, 24 * KB)
        region("attn1", 160 * KB, 47 * KB + 512)
        region("ffn1_hi", 160 * KB, 24 * KB)
        region("ffn1w", 184 * KB, 23 * KB + 512)
        region("ffn1v", 120 * KB, 16 * KB)
        region("ffn1x", 54 * KB, 64 * KB)
        region("prep1", 160 * KB, 47 * KB + 512)

        X = sb("keep", "X", [P, SUB, D])
        XTH = sb("keep", "XTH", [P, T], R32)
        XTL = sb("keep", "XTL", [P, T], R32)
        IDN = sb("keep", "IDN", [P, P])
        PICK64 = sb("keep", "PICK64", [P, 64], R32)
        PICK8 = sb("keep", "PICK8", [16, 8], R32)
        COLS = sb("keep", "COLS", [P, 16])
        COL1 = sb("keep", "COL1", [P, 2 + 2 * U1])
        ST = sb("keep", "ST", [P, SB, 6])
        MV = sb("keep", "MV", [P, SB, 2])
        VE = sb("keep", "VE", [P, SB])
        SD = sb("keep", "SD", [P, SB])
        RS = sb("keep", "RS", [P, SB])
        STAGE = sb("keep", "STAGE", [P, 64 + 8])

        WUL_RAW = nc.alloc_sbuf_tensor_at("WUL_RAW", [P, E0 * 64 + 64], F32, offset=place["ffn0_lo"][0])
        WUL = sb("ffn0_lo", "WUL", [P, E0 * 64 + 64], R32)
        WDL_RAW = nc.alloc_sbuf_tensor_at("WDL_RAW", [P, UN0, D], F32, offset=place["ffn0_lo"][0])
        WDL = sb("ffn0_lo", "WDL", [P, UN0, D], R32)
        WUH = sb("ffn0_hi", "WUH", [P, E0 * 64 + 64], R32)
        WDH = sb("ffn0_hi", "WDH", [P, UN0, D], R32)
        CWT = sb("gates", "CWT", [P, T], R32)
        SU = [sb("work", f"SU{i}", [P, TB]) for i in range(2)]
        HF = [sb("work", f"HF{i}", [P, TB]) for i in range(3)]
        HH = [sb("work", f"HH{i}", [P, TB], R32) for i in range(3)]
        HL = [sb("work", f"HL{i}", [P, TB], R32) for i in range(3)]
        YF = sb("work", "YF", [P, TB])
        PICKW = sb("work", "PICKW", [P, E0, 64], R32)

        XN = sb("attn0", "XN", [P, SB, D])
        Z = sb("attn0", "Z", [P, SB, D])
        XF = sb("attn0", "XF", [P, N])
        ZF = sb("attn0", "ZF", [P, N])
        ZTH = sb("attn0", "ZTH", [P, N], R32)
        ZTL = sb("attn0", "ZTL", [P, N], R32)
        V = sb("attn0", "V", [P, SB, HV])
        w = "attn0w"
        WZR = nc.alloc_sbuf_tensor_at("WZR", [P, 2 * P + 2 * HV], F32, offset=place[w][0])
        WZL = sb(w, "WZL", [P, 2 * P + 2 * HV], R32)
        WZH = sb(w, "WZH", [P, 2 * P + 2 * HV], R32)
        WO0 = sb(w, "WO0", [P, H1, D])
        CEN = sb(w, "CEN", [P, E0])
        COS = sb(w, "COS", [P, N])
        SIN = sb(w, "SIN", [P, N])
        BVB = sb(w, "BVB", [P, HV])
        BOB = sb(w, "BOB", [P, D])
        L2W = sb(w, "L2W", [P, D])
        L2B = sb(w, "L2B", [P, D])
        EBB = sb(w, "EBB", [P, E0])
        PEB = sb(w, "PEB", [P, NREL])
        BIAS = sb(w, "BIAS", [P, GROUP])
        ROUT0 = place[w][0]
        SIG = sb(w, "SIG", [P, SB, E0])
        BI = sb(w, "BI", [P, SB, E0])
        CUT = sb(w, "CUT", [P, SB, E0])
        CS = sb(w, "CS", [P, SB, 2 * E0], R32)
        TOP8 = sb(w, "TOP8", [P, SB, 8])
        WS = sb(w, "WS", [P, 3, SB])
        QA = sb(w, "QA", [P, N])
        QB = sb(w, "QB", [P, N])
        G = sb(w, "G", [P, H1, N])
        AT = sb(w, "AT", [P, SB, P])
        TMP = sb(w, "TMP", [P, SB, GROUP])
        LK = sb(w, "LK", [P, SB, 32])
        KV = sb(w, "KV", [P, HV])
        QQ = sb(w, "QQ", [P, N])
        OG = sb(w, "OG", [P, H1, N])
        YT = sb(w, "YT", [P, SB, D])
        DIST = nc.alloc_sbuf_tensor_at("DIST", [P, GROUP, NREL], F32, offset=ROUT0)
        PROD = nc.alloc_sbuf_tensor_at("PROD", [P, GROUP, NREL], F32, offset=ROUT0 + 9 * KB)

        XN1 = sb("prep1", "XN1", [P, SB, D])
        XF1 = sb("prep1", "XF1", [P, N])
        XFP = sb("prep1", "XFP", [P, N])
        PF = sb("prep1", "PF", [P, N])
        PH = sb("prep1", "PH", [P, N], R32)
        PL = sb("prep1", "PL", [P, N], R32)
        WV1H = sb("prep1", "WV1H", [P, D], R32)
        WV1L = sb("prep1", "WV1L", [P, D], R32)
        WV1 = sb("prep1", "WV1", [P, D])
        GW = sb("prep1", "GW", [P, E1])
        GBB = sb("prep1", "GBB", [P, E1])
        BVB1 = sb("prep1", "BVB1", [P, D])
        LG = sb("prep1", "LG", [P, SB, 16])
        TOP2 = sb("prep1", "TOP2", [P, SB, 8])
        SEL2 = sb("prep1", "SEL2", [P, SB, 8])
        CUT2 = sb("prep1", "CUT2", [P, SB, 16])
        MASK2 = sb("prep1", "MASK2", [P, SB, E1])
        SH = sb("prep1", "SH", [P, SB, E1])
        EX = sb("prep1", "EX", [P, SB, E1])
        GM = sb("prep1", "GM", [P, SB, E1])
        GSUM = sb("prep1", "GSUM", [P, 2, SB])
        GATE = sb("prep1", "GATE", [P, SB, E1])
        GS = sb("keep", "GS", [P, SUB, 2 * E1], R32)
        V1 = sb("v_all", "V1", [P, NG, SB, HG, DK])
        L = [sb("attn1b", f"L{i}", [P, HG, N], R32) for i in range(2)]
        R = [sb("attn1", f"R{i}", [P, N], R32) for i in range(2)]
        EX1 = [sb("attn1b", f"EX1{i}", [P, 2 * TB]) for i in range(4)]
        VA = [sb("attn1", f"VA{i}", [P, SB, HG, 32]) for i in range(2)]
        MX = [sb("attn1", f"MX{i}", [P, 2, HG, 4, 2]) for i in range(2)]
        MN = [sb("attn1", f"MN{i}", [P, 2, HG * 4]) for i in range(2)]
        MH = [sb("attn1", f"MH{i}", [HG * 4, P], R32) for i in range(2)]
        ML = [sb("attn1", f"ML{i}", [HG * 4, P], R32) for i in range(2)]
        OSB = [sb("attn1b", f"OSB{i}", [P, N]) for i in range(2)]
        F1 = E1 * 2 * P
        W1R = nc.alloc_sbuf_tensor_at("W1R", [P, 2, F1], F32, offset=place["ffn1_lo"][0])
        W1L = sb("ffn1_lo", "W1L", [P, 2, F1], R32)
        W2R = nc.alloc_sbuf_tensor_at("W2R", [P, U1, D], F32, offset=place["ffn1_lo"][0])
        W2L = sb("ffn1_lo", "W2L", [P, U1, D], R32)
        W1H = sb("ffn1_hi", "W1H", [P, 2, F1], R32)
        W2H = sb("ffn1_hi", "W2H", [P, U1, D], R32)
        WO1 = sb("ffn1w", "WO1", [P, D])
        OT = sb("ffn1v", "OT", [P, 2 * HG, NI])
        DT = sb("ffn1x", "DT", [P, 2 * HG, NI])
        B2R = sb("ffn1w", "B2R", [16, D])
        B2H = sb("ffn1w", "B2H", [16, D], R32)
        B2L = sb("ffn1w", "B2L", [16, D], R32)
        S1 = [sb("ffn1w", f"S1{i}", [P, TB]) for i in range(2)]
        AH = [sb("ffn1w", f"AH{i}", [P, TB]) for i in range(2)]
        HF1 = [sb("ffn1w", f"HF1{i}", [P, TB]) for i in range(2)]
        HH1 = [sb("ffn1v", f"HH1{i}", [P, TB], R32) for i in range(3)]
        HL1 = [sb("ffn1x", f"HL1{i}", [P, TB], R32) for i in range(3)]
        GSS = sb("ffn1v", "GSS", [P, 4, 2 * E1], R32)
        GTT = sb("ffn1v", "GTT", [16, TB], R32)
        REC = sb("ffn1w", "REC", [P, TB])
        ON = sb("ffn1w", "ON", [P, TB])
        Y2 = sb("ffn1w", "Y2", [P, TB])
        FIN = sb("ffn1x", "FIN", [P, 4, D])

        phd = nc.dram_tensor("phd", [NG * 32, N], F32)
        pld = nc.dram_tensor("pld", [NG * 32, N], F32)
        od = nc.dram_tensor("od", [NG * HG, 32, N], F32)
        md = [nc.dram_tensor(f"md{i}", [2, 2, HG, TB], F32) for i in range(2)]

        PA, PB, PC, PD = [ctx.enter_context(nc.psum_tensor(n, [P, 2 * TB], F32)) for n in ("PA", "PB", "PC", "PD")]

        def bank(i):
            t = (PA, PB, PC, PD)[i // 2]
            return t[:, TB * (i % 2):TB * (i % 2) + TB]

        block = ctx.enter_context(nc.Block())

        def before(p, k, units):
            return p - k if p >= k else max(u for u in range(units) if u % k == p) - units

        def wu_cols(c):
            w = PAIRS // WCH * P
            return slice(w * c, w * c + w + (64 if c == WCH - 1 else 0))

        def wd_units(c):
            return slice(PAIRS // WCH * c, PAIRS // WCH * (c + 1))

        def w1_cols(c):
            return slice(U1 // WCH * P * c, U1 // WCH * P * (c + 1))

        def w2_units(c):
            return slice(U1 // WCH * c, U1 // WCH * (c + 1))

        def seq_of(at):
            idx, kind = at
            if kind == "pro":
                return ("turn", 0, 0) if idx == PRO_T0 else ("max", idx - (idx > PRO_T0), 0)
            if idx < CARRY:
                return "max", MAXIMA - CARRY + idx, 0
            if kind == "end" or idx == T1:
                return "turn", 1, 0
            if idx == T0:
                return "turn", 0, 1
            return "max", idx - CARRY - (idx > T1) - (idx > T0), 1

        def slot_bank(at):
            return bank(4 + (at[0] + (0 if at[1] == "pro" else PRO)) % 3)

        def ready(e, name, n=0, c=0):
            e.wait_ge(sem[name], n + (c + 1))

        def dmas(e, name, n):
            e.wait_ge(sem[name], 16 * n)

        def counted(e, name, n, c=0):
            e.wait_ge(sem[name], n + (c + 1 + CREDIT))

        def mm3(out, w, x, start, stop):
            nc.tensor.matmul(out, w[0], x[0], start=start, stop=False)
            nc.tensor.matmul(out, w[0], x[1], start=False, stop=False)
            return nc.tensor.matmul(out, w[1], x[0], start=False, stop=stop)

        consts = (
            (IDN[:], a["c_ident"]), (COLS[:], a["cols0"]), (WZR[:], a["wz"]), (CEN[:], a["centroids"]),
            (EBB[:], a["expert_biases"].partition_broadcast(P)),
            (DIST[:].rearrange("p i r -> p (i r)"), a["c_dist"]), (PEB[:], a["pos_emb"].partition_broadcast(P)),
            (COS[:], a["c_cos"]), (SIN[:], a["c_sin"]), (STAGE[:, 0:64], a["c_pick64"]),
            (STAGE[0:16, 64:72], a["c_pick8"]), (BVB[:], a["bv0"].partition_broadcast(P)),
            (BOB[:], a["bo0"].partition_broadcast(P)), (L2W[:], a["ln2_w"].partition_broadcast(P)),
            (L2B[:], a["ln2_b"].partition_broadcast(P)), (WO0[:], a["wo0"].rearrange("(h p) d -> p h d", p=P)),
            (COL1[:], a["cols1"]),
        )

        def ready_apart(e, name, n=0, c=0):
            e.wait_ge(sem[name], n + (c + 1))
            e.sem_inc(sem["passed"], 1)

        @block.sync
        def _(sp):
            sp.sem_inc(sem["ph_w"], 16)
            sp.sem_inc(sem["m_w"], 64)
            sp.sem_inc(sem["out_s"], 16)
            for name in OD_W:
                sp.sem_inc(sem[name], 16)
            for b in range(B):
                sp.dma_start(X[:, SB * b:SB * b + SB, :],
                             a["x"][b].rearrange("(s p) d -> p s d", p=P)).then_inc(sem["x_in"], 16)
                if b == 0:
                    for dst, src in consts:
                        sp.dma_start(dst, src).then_inc(sem["c_in"], 16)
            sp.dma_start(WUL_RAW[:], a["w_up"]).then_inc(sem["w_in"], 16)
            sp.dma_start(WDL_RAW[:, 0:PAIRS, :], a["w_down"].rearrange("(u p) d -> p u d", p=P)).then_inc(sem["w_in"], 16)
            sp.dma_start(WDL_RAW[0:64, PAIRS, :], a["ws_down"]).then_inc(sem["w_in"], 16)
            with sp.Fori(0, B) as b:
                ready(sp, "qr", b)
                sp.dma_start(QQ[64:96, :], QA[0:32, :]).then_inc(sem["qqd"], 16)
            counted(sp, "d_x", 0, NT - 1)
            sp.dma_start(WV1[:], a["wv1"]).then_inc(sem["w2_in"], 16)
            sp.dma_start(GW[:], a["gate_w"]).then_inc(sem["w2_in"], 16)
            sp.dma_start(GBB[:], a["gate_b"].partition_broadcast(P)).then_inc(sem["w2_in"], 16)
            sp.dma_start(BVB1[:], a["bv1"].partition_broadcast(P)).then_inc(sem["w2_in"], 16)
            sp.dma_start(W1R[:, 0, :], a["w1"]).then_inc(sem["w2_in"], 16)
            sp.dma_start(W1R[:, 1, :], a["w0"]).then_inc(sem["w2_in"], 16)
            sp.dma_start(W2R[:], a["w2"].rearrange("(u p) d -> p u d", p=P)).then_inc(sem["w2_in"], 16)
            with sp.Fori(0, B) as b:
                ready(sp, "pl", b)
                sp.dma_start(phd[bass.ds(b * P, P), :], PH[:].bitcast(F32)).then_inc(sem["ph_w"], 16)
                sp.dma_start(pld[bass.ds(b * P, P), :], PL[:].bitcast(F32)).then_inc(sem["ph_w"], 16)
            sp.wait_ge(sem["ph_w"], 32 * B + 16)
            ready(sp, "l_zero", 0, 5)

            for par in range(2):
                for j in range(HG):
                    sp.dma_start(L[par][MR + j:MR + 2 * HG:HG, j, :].bitcast(F32), R[par][0:2, :].bitcast(F32)).then_inc(sem["lr"], 16)
            dmas(sp, "lr", 2 * HG)

            def load_lr(g, par):
                for r, (l, q) in enumerate(((phd, phd), (phd, pld), (pld, phd))):
                    sp.dma_start(R[par][HG * DK * r:HG * DK * (r + 1), :].bitcast(F32),
                                 q[bass.ds(g * 32, 32), :]).then_inc(sem["lr"], 16)
                    for j in range(HG):
                        rows = slice(HG * DK * r + DK * j, HG * DK * r + DK * j + DK)
                        sp.dma_start(L[par][rows, j, :].bitcast(F32), l[bass.ds(g * 32 + j * DK, DK), :]).then_inc(sem["lr"], 16)

            def maxima(g, half, par, slot):
                e = 2 * g + half
                counted(sp, "red", slot)
                sp.dma_start(md[half][par, 0].rearrange("j (c q) -> (j c) q", q=P), MH[half][:].bitcast(F32)).then_inc(sem["m_w"], 16)
                sp.dma_start(md[half][par, 1].rearrange("j (c q) -> (j c) q", q=P), ML[half][:].bitcast(F32)).then_inc(sem["m_w"], 16)
                sp.wait_ge(sem["m_w"], e * 32 + 96)
                sp.dma_start(R[par][MR:MR + 2 * HG, TB * half:TB * half + TB].bitcast(F32),
                             md[half][par].rearrange("x j q -> (x j) q")).then_inc(sem["m_r"], 16)

            def store_out(g, par):
                counted(sp, "osb", g * 2, 1)
                sp.dma_start(od[bass.ds(g * HG, HG)].rearrange("h r q -> (h r) q"), OSB[par][:]).then_inc(sem[OD_W[par]], 16)

            load_lr(0, 0)
            maxima(0, 0, 0, PRO_T0)
            with sp.Fori(0, NG // 2 - 1) as i:
                for par in range(2):
                    sp.wait_ge(sem["av"], (i * 2 + par) * 16 + AV0)
                    load_lr(i * 2 + (par + 1), 1 - par)
                    maxima(i * 2 + par, 1, par, (i * 2 + par) * SLOTS + (PRO + T1))
                    maxima(i * 2 + (par + 1), 0, 1 - par, (i * 2 + par) * SLOTS + (PRO + T0))
                    store_out(i * 2 + par, par)
            sp.wait_ge(sem["av"], (NG - 2) * 16 + AV0)
            load_lr(NG - 1, 1)
            maxima(NG - 2, 1, 0, (NG - 2) * SLOTS + PRO + T1)
            maxima(NG - 1, 0, 1, (NG - 2) * SLOTS + PRO + T0)
            store_out(NG - 2, 0)
            maxima(NG - 1, 1, 1, (NG - 1) * SLOTS + PRO + CARRY)
            store_out(NG - 1, 1)
            sp.wait_ge(sem["av"], NG * 16 + CREDIT)
            sp.dma_start(WO1[:], a["wo1"]).then_inc(sem["w2_in"], 16)
            sp.dma_start(B2R[:], a["b2"]).then_inc(sem["w2_in"], 16)
            for name in OD_W:
                sp.wait_ge(sem[name], NG // 2 * 16 + 16)
            with sp.Fori(0, NT) as n:
                sp.wait_ge(sem["on"], n + 1)
                for t, x in ((OT, 0), (DT, DK)):
                    for h in range(2 * HG):
                        sp.dma_start(t[:, h, :], od[bass.ds(n * (2 * HG) + h, 1), x:x + DK, :].rearrange(
                            "h d (c i) -> c (h d) i", i=NI)).then_inc(sem["ot_in"], 16)
                counted(sp, "fin", n)
                sp.dma_start(out[bass.ds(n * TB, TB), :].rearrange("(s p) d -> p s d", p=P), FIN[:]).then_inc(sem["out_s"], 16)
            dmas(sp, "out_s", NT + 1)

        @block.gpsimd
        def _(pool):
            for name in ("xtl", "extl", "on"):
                pool.sem_inc(sem[name], 1)
            with pool.Fori(0, B) as b:
                ready(pool, "xf", b)
                pool.tensor_copy(XTH[:, bass.ds(b * N, N)], XF[:]).then_inc(sem["xth"], 1)
                ready(pool, "xth", b)
                pool.tensor_tensor(XTL[:, bass.ds(b * N, N)], XF[:], XTH[:, bass.ds(b * N, N)], ALU.subtract).then_inc(sem["xtl"], 1)
            ready(pool, "xr", 0, B - 1)
            for c in range(WCH):
                es = slice(E0 // WCH * c, E0 // WCH * (c + 1))
                pool.tensor_copy(PICKW[:, es, :], PICK64[:, es].unsqueeze(2).to_broadcast([P, E0 // WCH, 64])
                                 ).then_inc(sem["pickw"], 1)
            with pool.Fori(0, B) as b:
                ready(pool, "exf", b)
                pool.tensor_copy(XTH[:, bass.ds(b * N, N)], XF1[:]).then_inc(sem["exth"], 1)
                ready(pool, "exth", b)
                pool.tensor_tensor(XTL[:, bass.ds(b * N, N)], XF1[:], XTH[:, bass.ds(b * N, N)], ALU.subtract).then_inc(sem["extl"], 1)
            ready(pool, "pl", 0, B - 1)
            pool.wait_ge(sem["ph_w"], 32 * B + 16)
            ready(pool, "ve", 0, B - 1)
            for t, v in ((L[0], 0.0), (L[1], 0.0), (R[0], 1.0), (R[1], 1.0), (VA[0], 1.0), (VA[1], 1.0)):
                pool.memset(t[:].bitcast(F32), v).then_inc(sem["l_zero"], 1)
            ready(pool, "l_zero", 0, 5)

            def value_columns(g, par):
                pool.wait_ge(sem["av"], g * 16 + (AV0 - 16))
                pool.tensor_copy(VA[par][:, :, :, 0:DK],
                                 V1[:, bass.ds(g, 1), :, :, :].rearrange("p g s j d -> p (g s) j d")).then_inc(sem["va"], 1)

            value_columns(0, 0)
            with pool.Fori(0, NG // 2 - 1) as i:
                for par in range(2):
                    value_columns(i * 2 + (par + 1), 1 - par)
            value_columns(NG - 1, 1)
            with pool.Fori(0, NT) as n:
                pool.wait_ge(sem["gstp"], n + 1)
                pool.tensor_copy(GSS[:], GS[:, bass.ds(n * 4, 4), :]).then_inc(sem["gss"], 1)
                ready(pool, "rec", n)
                pool.wait_ge(sem["pj"], n + 1)
                pool.tensor_tensor(ON[:], OT[:].rearrange("p h i -> p (h i)"), REC[:], ALU.mult).then_inc(sem["on"], 1)

        def norm_stats(e, pre, x_of, n):
            for s in range(SB):
                last = nc.vector.bn_stats(ST[:, s, :], x_of(s))
            last.then_inc(sem[pre + "_own"], 1)
            ready_apart(e, pre + "_own", n * 3, 0)
            for s in range(SB):
                last = nc.vector.bn_aggr(MV[:, s, :], ST[:, s, :])
            last.then_inc(sem[pre + "_own"], 1)
            ready(e, pre + "_own", n * 3, 1)
            nc.vector.tensor_scalar(VE[:], MV[:, :, 1], EPS, None, ALU.add).then_inc(sem[pre + "_var"], 1)

        def norm_apply(e, pre, x_of, out_of, done, n):
            ready(e, pre + "_std", n)
            nc.vector.reciprocal(RS[:], SD[:]).then_inc(sem[pre + "_own"], 1)
            ready(e, pre + "_own", n * 3, 2)
            for s in range(SB):
                last = nc.vector.tensor_scalar(out_of(s), x_of(s), MV[:, s, 0:1], RS[:, s:s + 1],
                                               ALU.subtract, ALU.mult)
            last.then_inc(sem[done], 1)

        def x_sub(b, s):
            return X[:, bass.ds(b * SB + s, 1), :].rearrange("p s d -> p (s d)")

        @block.vector
        def _(dve):
            for name in ("hf", "lo", "d_x", "red", "ah", "hf1", "lo1", "fin"):
                dve.sem_inc(sem[name], CREDIT)
            tt, ts, cp = nc.vector.tensor_tensor, nc.vector.tensor_scalar, nc.vector.tensor_copy
            dmas(dve, "c_in", len(consts))
            tt(PROD[:], DIST[:], PEB[:].unsqueeze(1).to_broadcast([P, GROUP, NREL]), ALU.mult).then_inc(sem["peb_m"], 1)
            cp(PICK64[:], STAGE[:, 0:64])
            cp(PICK8[:], STAGE[0:16, 64:72])
            cp(WZH[:], WZR[:]).then_inc(sem["wz_h"], 1)
            nc.vector.memset(AT[:], 0.0)
            ready(dve, "peb_m")
            nc.vector.tensor_reduce(BIAS[:], PROD[:], AX.X, ALU.add).then_inc(sem["bias_q"], 1)
            ready(dve, "wz_h")
            tt(WZL[:], WZR[:], WZH[:], ALU.subtract).then_inc(sem["wz_l"], 1)
            ready(dve, "bias_q")
            ready(dve, "wz_l")

            with dve.Fori(0, B) as b:
                dve.wait_ge(sem["x_in"], b * 16 + 16)
                norm_stats(dve, "x", lambda s: x_sub(b, s), b)
                norm_apply(dve, "x", lambda s: x_sub(b, s), lambda s: XN[:, s, :], "xn", b)
                ready(dve, "xn", b)
                norm_stats(dve, "z", lambda s: XN[:, s, :], b)
                norm_apply(dve, "z", lambda s: XN[:, s, :], lambda s: Z[:, s, :], "z", b)
                ready(dve, "zt", b)
                ts(ZF[:], PB[:], COLS[:, 0:1], COLS[:, 1:2], ALU.mult, ALU.add).then_inc(sem["zf"], 1)
                ready(dve, "zth", b)
                tt(ZTL[:], ZF[:], ZTH[:], ALU.subtract).then_inc(sem["ztl"], 1)
                ready(dve, "sig", b)
                tt(BI[:], PC[:, 0:SB * E0].rearrange("p (s e) -> p s e", e=E0),
                   EBB[:].unsqueeze(1).to_broadcast([P, SB, E0]), ALU.add).then_inc(sem["bi"], 1)
                ready_apart(dve, "bi", b)
                for s in range(SB):
                    last = nc.vector.max(TOP8[:, s, :], BI[:, s, :])
                last.then_inc(sem["route"], 1)
                ready_apart(dve, "route", b * 9, 0)
                for s in range(SB):
                    last = nc.vector.match_replace(out=CUT[:, s, :], in_to_replace=TOP8[:, s, :],
                                                   in_values=BI[:, s, :], imm_value=LOWEST)
                last.then_inc(sem["route"], 1)
                ready(dve, "route", b * 9, 1)
                tt(CUT[:], CUT[:], BI[:], ALU.not_equal).then_inc(sem["route"], 1)
                ready(dve, "route", b * 9, 2)
                tt(SIG[:], SIG[:], CUT[:], ALU.mult).then_inc(sem["route"], 1)
                ready(dve, "route", b * 9, 3)
                nc.vector.tensor_reduce(WS[:, 0, :], SIG[:], AX.X, ALU.add).then_inc(sem["route"], 1)
                ready(dve, "route", b * 9, 4)
                ts(WS[:, 1, :], WS[:, 0, :], 1e-8, None, ALU.add).then_inc(sem["route"], 1)
                ready(dve, "route", b * 9, 5)
                nc.vector.reciprocal(WS[:, 2, :], WS[:, 1, :]).then_inc(sem["route"], 1)
                ready(dve, "route", b * 9, 6)
                tt(BI[:], SIG[:], WS[:, 2, :].unsqueeze(2).to_broadcast([P, SB, E0]), ALU.mult).then_inc(sem["route"], 1)
                ready(dve, "route", b * 9, 7)
                cp(CS[:, :, 0:E0], BI[:]).then_inc(sem["route"], 1)
                ready(dve, "route", b * 9, 8)
                tt(CS[:, :, E0:2 * E0], BI[:], CS[:, :, 0:E0], ALU.subtract).then_inc(sem["cs"], 1)
                ready(dve, "qa", b)
                ts(QA[:], QA[:], COLS[:, 4:5], COLS[:, 5:6], ALU.mult, ALU.add).then_inc(sem["rope"], 1)
                ready(dve, "qb", b)
                ts(QB[:], QB[:], COLS[:, 6:7], COLS[:, 7:8], ALU.mult, ALU.add).then_inc(sem["rope"], 1)
                ready(dve, "rope", b * 4, 0)
                tt(QA[:], QA[:], COS[:], ALU.mult).then_inc(sem["rope"], 1)
                ready(dve, "rope", b * 4, 1)
                tt(QB[:], QB[:], SIN[:], ALU.mult).then_inc(sem["rope"], 1)
                ready(dve, "rope", b * 4, 2)
                ready(dve, "rope", b * 4, 3)
                tt(QA[:], QA[:], QB[:], ALU.add).then_inc(sem["qr"], 1)
                ready(dve, "v1p", b)
                tt(V[:, 0:4, :], PD[:].rearrange("p (s e) -> p s e", e=HV),
                   BVB[:].unsqueeze(1).to_broadcast([P, 4, HV]), ALU.add).then_inc(sem["vb1"], 1)
                ready(dve, "v2p", b)
                tt(V[:, 4:8, :], PA[:].rearrange("p (s e) -> p s e", e=HV),
                   BVB[:].unsqueeze(1).to_broadcast([P, 4, HV]), ALU.add).then_inc(sem["vb2"], 1)
                ready(dve, "lkt", b)
                cp(LK[:], PA[:, 0:SB * 32].rearrange("p (s c) -> p s c", c=32)).then_inc(sem["lk"], 1)
                ready(dve, "st", b)
                for h in range(2):
                    rows = slice(GROUP * h, GROUP * h + GROUP)
                    last = nc.vector.scalar_tensor_tensor(
                        out=TMP[rows, :, :], in0=PD[rows, :].rearrange("p (s i) -> p s i", i=P)[:, :, rows],
                        scalar=1.0 / GROUP, in1=BIAS[rows, :].unsqueeze(1).to_broadcast([GROUP, SB, GROUP]),
                        op0=ALU.mult, op1=ALU.add)
                last.then_inc(sem["tb"], 1)
                ready(dve, "tb", b)
                for h in range(2):
                    rows = slice(GROUP * h, GROUP * h + GROUP)
                    last = nc.vector.scalar_tensor_tensor(out=AT[rows, :, rows], in0=TMP[rows, :, :], scalar=0.0,
                                                          in1=TMP[rows, :, :], op0=ALU.max, op1=ALU.mult)
                last.then_inc(sem["att"], 1)
                for h, (ot, g, pt) in enumerate((("ot0", "g0", PB), ("ot1", "g1", PC))):
                    ready(dve, ot, b)
                    ready(dve, g, b)
                    tt(OG[:, h, :], pt[:], G[:, h, :], ALU.mult).then_inc(sem[("og0", "og1")[h]], 1)
                ready(dve, "yp", b)
                tt(YT[:], PD[:].rearrange("p (s d) -> p s d", d=D), BOB[:].unsqueeze(1).to_broadcast([P, SB, D]),
                   ALU.add).then_inc(sem["y"], 1)
                ready(dve, "y", b)
                norm_stats(dve, "y", lambda s: YT[:, s, :], b)
                norm_apply(dve, "y", lambda s: YT[:, s, :], lambda s: YT[:, s, :], "yn", b)
                ready(dve, "yn", b)
                tt(YT[:], YT[:], L2W[:].unsqueeze(1).to_broadcast([P, SB, D]), ALU.mult).then_inc(sem["yw"], 1)
                ready(dve, "yw", b)
                tt(YT[:], YT[:], L2B[:].unsqueeze(1).to_broadcast([P, SB, D]), ALU.add).then_inc(sem["yb"], 1)
                ready(dve, "yb", b)
                tt(X[:, bass.ds(b * SB, SB), :], X[:, bass.ds(b * SB, SB), :], YT[:], ALU.add).then_inc(sem["xr"], 1)

            for c in range(WCH):
                ready(dve, "wu_h", 0, c)
                tt(WUL[:, wu_cols(c)], WUL_RAW[:, wu_cols(c)], WUH[:, wu_cols(c)], ALU.subtract).then_inc(sem["wu_l"], 1)
                ready(dve, "wd_h", 0, c)
                tt(WDL[:, wd_units(c), :], WDL_RAW[:, wd_units(c), :], WDH[:, wd_units(c), :],
                   ALU.subtract).then_inc(sem["wd_l"], 1)
            ready(dve, "wd_h", 0, WCH)
            tt(WDL[0:64, PAIRS, :], WDL_RAW[0:64, PAIRS, :], WDH[0:64, PAIRS, :], ALU.subtract).then_inc(sem["wd_l"], 1)

            with dve.Fori(0, NT) as n:
                for p in range(UN0 + 2):
                    if p >= 2:
                        q = p - 2
                        M = P if q < PAIRS else 64
                        counted(dve, "hi", n * UN0, q)
                        counted(dve, "down", n * UN0, before(q, 3, UN0))
                        tt(HL[q % 3][0:M, :], HF[q % 3][0:M, :], HH[q % 3][0:M, :], ALU.subtract).then_inc(sem["lo"], 1)
                    if p < UN0:
                        M = P if p < PAIRS else 64
                        counted(dve, "silu", n * UN0, p)
                        counted(dve, "lo", n * UN0, before(p, 3, UN0))
                        if p < PAIRS:
                            counted(dve, "bc", n * PAIRS, p)
                            tt(HF[p % 3][:], SU[p % 2][:], bank(3 + p % 2), ALU.mult).then_inc(sem["hf"], 1)
                        else:
                            cp(HF[p % 3][0:M, :], SU[p % 2][0:M, :]).then_inc(sem["hf"], 1)
                ready(dve, "ytp", n)
                xs = X[:, bass.ds(n * 4, 4), :].rearrange("p s d -> p (s d)")
                tt(xs, xs, bank(6), ALU.add).then_inc(sem["d_x"], 1)

            dmas(dve, "w2_in", 7)
            counted(dve, "d_x", 0, NT - 1)
            cp(WV1H[:], WV1[:]).then_inc(sem["wz_h"], 1)
            nc.vector.memset(LG[:, :, E1:16], LOWEST)
            nc.vector.memset(SEL2[:, :, 2:8], LOWEST)
            ready(dve, "wz_h", 0, 1)
            tt(WV1L[:], WV1[:], WV1H[:], ALU.subtract).then_inc(sem["wz_l"], 1)
            with dve.Fori(0, B) as b:
                norm_stats(dve, "e", lambda s: x_sub(b, s), b)
                norm_apply(dve, "e", lambda s: x_sub(b, s), lambda s: XN1[:, s, :], "exn", b)
                ready(dve, "lg", b)
                tt(LG[:, :, 0:E1], PD[:, 0:SB * E1].rearrange("p (s e) -> p s e", e=E1),
                   GBB[:].unsqueeze(1).to_broadcast([P, SB, E1]), ALU.add).then_inc(sem["route2"], 1)
                ready_apart(dve, "route2", b * 10, 0)
                for s in range(SB):
                    last = nc.vector.max(TOP2[:, s, :], LG[:, s, 0:14])
                last.then_inc(sem["route2"], 1)
                ready(dve, "route2", b * 10, 1)
                cp(SEL2[:, :, 0:2], TOP2[:, :, 0:2]).then_inc(sem["route2"], 1)
                tt(SH[:], LG[:, :, 0:E1], TOP2[:, :, 0:1].to_broadcast([P, SB, E1]), ALU.subtract).then_inc(sem["shift"], 1)
                ready_apart(dve, "route2", b * 10, 2)
                for s in range(SB):
                    last = nc.vector.match_replace(out=CUT2[:, s, 0:14], in_to_replace=SEL2[:, s, :],
                                                   in_values=LG[:, s, 0:14], imm_value=-LOWEST)
                last.then_inc(sem["route2"], 1)
                ready(dve, "route2", b * 10, 3)
                tt(MASK2[:], CUT2[:, :, 0:E1], LG[:, :, 0:E1], ALU.not_equal).then_inc(sem["route2"], 1)
                ready(dve, "route2", b * 10, 4)
                ready(dve, "ex", b)
                tt(GM[:], EX[:], MASK2[:], ALU.mult).then_inc(sem["route2"], 1)
                ready(dve, "route2", b * 10, 5)
                nc.vector.tensor_reduce(GSUM[:, 0, :], GM[:], AX.X, ALU.add).then_inc(sem["route2"], 1)
                ready(dve, "route2", b * 10, 6)
                nc.vector.reciprocal(GSUM[:, 1, :], GSUM[:, 0, :]).then_inc(sem["route2"], 1)
                ready(dve, "route2", b * 10, 7)
                tt(GATE[:], GM[:], GSUM[:, 1, :].unsqueeze(2).to_broadcast([P, SB, E1]), ALU.mult).then_inc(sem["route2"], 1)
                ready(dve, "route2", b * 10, 8)
                cp(GS[:, bass.ds(b * SB, SB), 0:E1], GATE[:]).then_inc(sem["route2"], 1)
                ready(dve, "route2", b * 10, 9)
                tt(GS[:, bass.ds(b * SB, SB), E1:2 * E1], GATE[:], GS[:, bass.ds(b * SB, SB), 0:E1],
                   ALU.subtract).then_inc(sem["gs"], 1)
                ready(dve, "pp", b)
                dve.wait_ge(sem["ph_w"], b * 32 + 16)
                ts(PF[:].rearrange("p (c i) -> p i c", i=NI), PB[:].rearrange("p (i c) -> p i c", i=NI),
                   COL1[:, 0:1], None, ALU.add).then_inc(sem["pf"], 1)
                ready(dve, "ph", b)
                tt(PL[:], PF[:], PH[:], ALU.subtract).then_inc(sem["pl"], 1)
                ready(dve, "vp", b)
                for g in range(HG):
                    x = 32 * g
                    last = tt(V1[:, bass.ds(b * HG + g, 1), :, :, :].rearrange("p g s j d -> p (g s) (j d)"),
                              PC[:].rearrange("p (s e) -> p s e", e=D)[:, :, x:x + 32],
                              BVB1[:, x:x + 32].unsqueeze(1).to_broadcast([P, SB, 32]), ALU.add)
                last.then_inc(sem["ve"], 1)

            def slot(x, idx, g, par):
                mb = slot_bank(idx)
                kind, u, ahead = seq_of(idx)
                gp = (par + ahead) % 2
                counted(dve, "mx", x)
                if kind == "max":
                    half, c4, j, h = u // 32, (u % 32) // 8, (u % 8) // 2, u % 2
                    nc.vector.tensor_reduce(MX[gp][:, half, j, c4, h:h + 1], mb, AX.X, ALU.max).then_inc(sem["red"], 1)
                    if u % 32 == 31:
                        counted(dve, "red", x)
                        nc.vector.tensor_reduce(MN[gp][:, half, :], MX[gp][:, half, :, :, :].rearrange("p j c h -> p (j c) h"),
                                                AX.X, ALU.max, negate=True).then_inc(sem["neg"], 1)
                else:
                    e = (g + ahead) * 2 + u
                    dve.wait_ge(sem["m_w"], e * 32 + 32)
                    cp(MH[u][:], mb[0:HG * 4, 0:P]).then_inc(sem["mhi"], 1)
                    ready(dve, "mhi", e)
                    tt(ML[u][:], mb[0:HG * 4, 0:P], MH[u][:], ALU.subtract).then_inc(sem["red"], 1)

            for idx in range(PRO):
                slot(idx, (idx, "pro"), 0, 0)
            with dve.Fori(0, NG // 2 - 1) as i:
                for par in range(2):
                    for idx in range(SLOTS):
                        slot((i * 2 + par) * SLOTS + (PRO + idx), (idx, "body"), i * 2 + par, par)
            for idx in range(SLOTS):
                slot((NG - 2) * SLOTS + PRO + idx, (idx, "body"), NG - 2, 0)
            for idx in range(SLOTS_END):
                slot((NG - 1) * SLOTS + PRO + idx, (idx, "end"), NG - 1, 1)

            dmas(dve, "w2_in", 9)
            for c in range(WCH):
                ready(dve, "w1_h", 0, c)
                tt(W1L[:, :, w1_cols(c)], W1R[:, :, w1_cols(c)], W1H[:, :, w1_cols(c)], ALU.subtract).then_inc(sem["w1_l"], 1)
                ready(dve, "w2_h", 0, c)
                tt(W2L[:, w2_units(c), :], W2R[:, w2_units(c), :], W2H[:, w2_units(c), :], ALU.subtract).then_inc(sem["w2_l"], 1)
            cp(B2H[:], B2R[:]).then_inc(sem["b2_h"], 1)
            ready(dve, "b2_h")
            tt(B2L[:], B2R[:], B2H[:], ALU.subtract).then_inc(sem["b2_l"], 1)
            with dve.Fori(0, NT) as n:
                u0 = n * U1
                for p in range(U1 + 1):
                    if p < U1:
                        counted(dve, "s1", u0, p)
                        counted(dve, "hf1", u0, before(p, 2, U1))
                        counted(dve, "h0", u0, p)
                        nc.vector.scalar_tensor_tensor(
                            out=AH[p % 2][:], in0=bank(2 + p % 2), scalar=COL1[:, 2 + p:3 + p], in1=S1[p % 2][:],
                            op0=ALU.add, op1=ALU.mult).then_inc(sem["ah"], 1)
                        counted(dve, "ah", u0, p)
                        counted(dve, "bg", n * E1, p // 2)
                        counted(dve, "lo1", u0, before(p, 2, U1))
                        tt(HF1[p % 2][:], AH[p % 2][:], bank((4, 7)[p // 2 % 2]), ALU.mult).then_inc(sem["hf1"], 1)
                    if p >= 1:
                        q = p - 1
                        counted(dve, "hi1", u0, q)
                        counted(dve, "dn1", u0, before(q, 3, U1))
                        tt(HL1[q % 3][:], HF1[q % 2][:], HH1[q % 3][:], ALU.subtract).then_inc(sem["lo1"], 1)
                    if p == 3:
                        dve.wait_ge(sem["ot_in"], (n + 1) * (2 * 2 * HG * 16))
                        dve.wait_ge(sem["on"], n + 1)
                        nc.vector.reciprocal(REC[:], DT[:].rearrange("p h i -> p (h i)")).then_inc(sem["rec"], 1)
                ready(dve, "ytp2", n)
                dve.wait_ge(sem["out_s"], n * 16 + 16)
                tt(FIN[:].rearrange("p s d -> p (s d)"), X[:, bass.ds(n * 4, 4), :].rearrange("p s d -> p (s d)"),
                   bank(6), ALU.add).then_inc(sem["fin"], 1)

        @block.scalar
        def _(act):
            for name in ("silu", "hi", "exq", "osb", "s1", "hi1"):
                act.sem_inc(sem[name], CREDIT)
            fn, copy = nc.scalar.activation, ACT.Copy
            dmas(act, "c_in", len(consts))
            with act.Fori(0, B) as b:
                ready(act, "x_var", b)
                fn(SD[:], VE[:], ACT.Sqrt).then_inc(sem["x_std"], 1)
                ready(act, "xt", b)
                act.wait_ge(sem["xtl"], b + 1)
                fn(XF[:], PA[:], copy).then_inc(sem["xf"], 1)
                ready(act, "z_var", b)
                fn(SD[:], VE[:], ACT.Sqrt).then_inc(sem["z_std"], 1)
                ready(act, "zf", b)
                fn(ZTH[:], ZF[:], copy).then_inc(sem["zth"], 1)
                ready(act, "aff", b)
                fn(SIG[:].rearrange("p s e -> p (s e)"), PC[:, 0:SB * E0], ACT.Sigmoid).then_inc(sem["sig"], 1)
                ready(act, "qp", b)
                fn(QA[:], PB[:], ACT.Silu, bias=COLS[:, 2:3]).then_inc(sem["qa"], 1)
                ready(act, "qs", b)
                fn(QB[:], PC[:], ACT.Silu, bias=COLS[:, 3:4]).then_inc(sem["qb"], 1)
                ready(act, "cst", b)
                fn(CWT[:, bass.ds(b * N, N)], PA[:], copy).then_inc(sem["cwt"], 1)
                ready(act, "vb1", b)
                fn(V[:, 0:4, :], V[:, 0:4, :], ACT.Silu).then_inc(sem["v1"], 1)
                ready(act, "vb2", b)
                fn(V[:, 4:8, :], V[:, 4:8, :], ACT.Silu).then_inc(sem["v2"], 1)
                ready(act, "g0p", b)
                fn(G[:, 0, :], PB[:], ACT.Silu, bias=COLS[:, 8:9]).then_inc(sem["g0"], 1)
                ready(act, "g1p", b)
                fn(G[:, 1, :], PC[:], ACT.Silu, bias=COLS[:, 9:10]).then_inc(sem["g1"], 1)
                ready(act, "kvp", b)
                fn(KV[32:64, :], PA[32:64, TB:TB + HV], copy, scale=1.0 / N).then_inc(sem["kv"], 1)
                ready(act, "y_var", b)
                fn(SD[:], VE[:], ACT.Sqrt).then_inc(sem["y_std"], 1)

            ready(act, "xr", 0, B - 1)
            act.wait_ge(sem["xtl"], B + 1)
            dmas(act, "w_in", 3)
            for c in range(WCH):
                fn(WUH[:, wu_cols(c)], WUL_RAW[:, wu_cols(c)], copy).then_inc(sem["wu_h"], 1)
                fn(WDH[:, wd_units(c), :], WDL_RAW[:, wd_units(c), :], copy).then_inc(sem["wd_h"], 1)
            fn(WDH[0:64, PAIRS, :], WDL_RAW[0:64, PAIRS, :], copy).then_inc(sem["wd_h"], 1)
            with act.Fori(0, NT) as n:
                for p in range(UN0 + 1):
                    if p < UN0:
                        M = P if p < PAIRS else 64
                        counted(act, "up", n * UN0, p)
                        counted(act, "hf", n * UN0, before(p, 2, UN0))
                        fn(SU[p % 2][0:M, :], bank(p % 3)[0:M, :], ACT.Silu).then_inc(sem["silu"], 1)
                    if p >= 1:
                        q = p - 1
                        M = P if q < PAIRS else 64
                        counted(act, "hf", n * UN0, q)
                        counted(act, "down", n * UN0, before(q, 3, UN0))
                        fn(HH[q % 3][0:M, :], HF[q % 3][0:M, :], copy).then_inc(sem["hi"], 1)
                counted(act, "down", n * UN0, UN0 - 1)
                fn(YF[:], bank(5), copy).then_inc(sem["yt"], 1)

            with act.Fori(0, B) as b:
                ready(act, "e_var", b)
                fn(SD[:], VE[:], ACT.Sqrt).then_inc(sem["e_std"], 1)
                ready(act, "ext", b)
                act.wait_ge(sem["extl"], b + 1)
                fn(XF1[:], PA[:], copy).then_inc(sem["exf"], 1)
                fn(XFP[:].rearrange("p (c i) -> p c i", i=NI), PA[:].rearrange("p (i c) -> p c i", i=NI),
                   copy).then_inc(sem["xfp"], 1)
                ready(act, "shift", b)
                fn(EX[:], SH[:], ACT.Exp).then_inc(sem["ex"], 1)
                ready(act, "pf", b)
                fn(PH[:], PF[:], copy).then_inc(sem["ph"], 1)

            def exps(s, k):
                for pair in range(2):
                    counted(act, "sc", s * 2, 2 * k + pair)
                    act.wait_ge(sem["av"], s + (k - 1 + AV0))
                    fn(EX1[(2 * k + pair) % 4][:], (PA, PB)[pair][:], ACT.Exp, scale=SCALE).then_inc(sem["exq"], 1)

            def out_half(g, i, k, par):
                act.wait_ge(sem["av"], g * 16 + (k + 1 + AV0))
                act.wait_ge(sem[OD_W[par]], i * 16 + 16)
                fn(OSB[par][:, TB * (k // 8):TB * (k // 8) + TB], bank(7), copy).then_inc(sem["osb"], 1)

            ready(act, "l_zero", 0, 5)
            exps(0, 0)
            with act.Fori(0, NG // 2 - 1) as i:
                for par in range(2):
                    for k in range(16):
                        exps((i * 2 + par) * 16, k + 1)
                        if k % 8 == 7:
                            out_half(i * 2 + par, i, k, par)
            for g in range(NG - 2, NG):
                for k in range(16):
                    if k < 15 or g < NG - 1:
                        exps(g * 16, k + 1)
                    if k % 8 == 7:
                        out_half(g, g // 2, k, g % 2)

            dmas(act, "w2_in", 9)
            counted(act, "red", (NG - 1) * SLOTS + PRO + CARRY)
            for c in range(WCH):
                fn(W1H[:, :, w1_cols(c)], W1R[:, :, w1_cols(c)], copy).then_inc(sem["w1_h"], 1)
                fn(W2H[:, w2_units(c), :], W2R[:, w2_units(c), :], copy).then_inc(sem["w2_h"], 1)
            with act.Fori(0, NT) as n:
                u0 = n * U1
                ready(act, "gstp", n, 1)
                fn(GTT[:], bank(6)[0:2 * E1, :], copy).then_inc(sem["gt"], 1)
                for p in range(U1 + 1):
                    if p < U1:
                        counted(act, "h1", u0, p)
                        counted(act, "ah", u0, before(p, 2, U1))
                        fn(S1[p % 2][:], bank(p % 2), ACT.Silu, bias=COL1[:, 2 + U1 + p:3 + U1 + p]).then_inc(sem["s1"], 1)
                    if p >= 1:
                        q = p - 1
                        counted(act, "hf1", u0, q)
                        counted(act, "dn1", u0, before(q, 3, U1))
                        fn(HH1[q % 3][:], HF1[q % 2][:], copy).then_inc(sem["hi1"], 1)
                counted(act, "dn1", u0, U1 - 1)
                fn(Y2[:], bank(5), ACT.Identity, bias=COL1[:, 1:2]).then_inc(sem["y2s"], 1)

        @block.tensor
        def _(pe):
            for name in ("up", "bc", "down", "sc", "mx", "h1", "h0", "bg", "dn1"):
                pe.sem_inc(sem[name], CREDIT)
            pe.sem_inc(sem["av"], AV0)
            pe.sem_inc(sem["gstp"], 1)
            pe.sem_inc(sem["pj"], 1)
            mm, tr = nc.tensor.matmul, nc.tensor.transpose
            ready(pe, "wz_l")
            ready(pe, "bias_q")

            with pe.Fori(0, B) as b:
                ready(pe, "xn", b)
                for s in range(SB):
                    last = tr(PA[:, P * s:P * s + P], XN[:, s, :], IDN[:])
                last.then_inc(sem["xt"], 1)
                ready(pe, "xf", b)
                for s in range(SB):
                    last = mm(PC[:, E0 * s:E0 * s + E0], XF[:, P * s:P * s + P], CEN[:], start=True, stop=True)
                last.then_inc(sem["aff"], 1)
                ready(pe, "z", b)
                for s in range(SB):
                    last = tr(PB[:, P * s:P * s + P], Z[:, s, :], IDN[:])
                last.then_inc(sem["zt"], 1)
                ready(pe, "zth", b)
                ready(pe, "ztl", b)

                def project(dst, c0, done):
                    for h in range(2):
                        c = slice(TB * h, TB * h + TB)
                        last = mm3(dst[:, c], (WZH[:, c0:c0 + P], WZL[:, c0:c0 + P]), (ZTH[:, c], ZTL[:, c]), True, True)
                    last.then_inc(sem[done], 1)

                def values(dst, s0, done):
                    c = slice(2 * P, 2 * P + HV)
                    for s in range(4):
                        t = slice(P * (s0 + s), P * (s0 + s) + P)
                        last = mm3(dst[:, HV * s:HV * s + HV], (ZTH[:, t], ZTL[:, t]), (WZH[:, c], WZL[:, c]), True, True)
                    last.then_inc(sem[done], 1)

                project(PB, 0, "qp")
                ready(pe, "bi", b)
                ready(pe, "sig", b)
                project(PC, P, "qs")
                values(PD, 0, "v1p")
                ready(pe, "cs", b)
                for s in range(SB):
                    last = tr(PA[:, P * s:P * s + P], CS[:, s, :].bitcast(F32), IDN[:])
                last.then_inc(sem["cst"], 1)
                ready(pe, "cwt", b)
                values(PA, 4, "v2p")
                ready(pe, "qa", b)
                project(PB, 2 * P + HV, "g0p")
                ready(pe, "qb", b)
                project(PC, 3 * P + HV, "g1p")
                dmas(pe, "c_in", len(consts))
                ready(pe, "qr", b)
                ready(pe, "vb2", b)
                for s in range(SB):
                    last = tr(PA[:, 32 * s:32 * s + 32], QA[96:128, P * s:P * s + P], IDN[96:128, 96:128])
                last.then_inc(sem["lkt"], 1)
                ready(pe, "vb1", b)
                pe.wait_ge(sem["qqd"], b * 16 + 16)
                for s in range(SB):
                    t = slice(P * s, P * s + P)
                    last = mm(PD[:, t], QA[64:96, t], QQ[64:96, t], start=True, stop=True)
                last.then_inc(sem["st"], 1)
                ready(pe, "lk", b)
                ready(pe, "v1", b)
                ready(pe, "v2", b)
                for s in range(SB):
                    last = mm(PA[32:64, TB:TB + HV], LK[:, s, :], V[:, s, :], start=(s == 0), stop=(s == SB - 1))
                last.then_inc(sem["kvp"], 1)
                ready(pe, "kv", b)
                ready(pe, "att", b)
                for h, (pt, g, done) in enumerate(((PB, "g0", "ot0"), (PC, "g1", "ot1"))):
                    ready(pe, g, b)
                    rows = slice(P * h, P * h + P)
                    for q in range(2):
                        o = pt[:, TB * q:TB * q + TB]
                        mm(o, KV[32:64, rows], QA[32:64, TB * q:TB * q + TB], start=True, stop=False)
                        for s in range(4):
                            last = mm(o[:, P * s:P * s + P], V[:, 4 * q + s, rows], AT[:, 4 * q + s, :],
                                      start=False, stop=(s == 3))
                    last.then_inc(sem[done], 1)
                ready(pe, "og0", b)
                ready(pe, "og1", b)
                for s in range(SB):
                    for h in range(H1):
                        last = mm(PD[:, P * s:P * s + P], OG[:, h, P * s:P * s + P], WO0[:, h, :],
                                  start=(h == 0), stop=(h == H1 - 1))
                last.then_inc(sem["yp"], 1)

            ready(pe, "xr", 0, B - 1)
            pe.wait_ge(sem["xtl"], B + 1)
            ready(pe, "cwt", 0, B - 1)
            with pe.Fori(0, NT) as n:
                xh, xl = XTH[:, bass.ds(n * TB, TB)], XTL[:, bass.ds(n * TB, TB)]
                for p in range(UN0 + LAG):
                    if p < UN0:
                        M = P if p < PAIRS else 64
                        if p % (PAIRS // WCH) == 0 and p < PAIRS:
                            ready(pe, "wu_l", 0, p // (PAIRS // WCH))
                            ready(pe, "pickw", 0, p // (PAIRS // WCH))
                        if M < P:
                            dmas(pe, "c_in", len(consts))
                        counted(pe, "silu", n * UN0, before(p, 3, UN0))
                        c = slice(P * p, P * p + M)
                        mm3(bank(p % 3)[0:M, :], (WUH[:, c], WUL[:, c]), (xh, xl), True, True).then_inc(sem["up"], 1)
                        if p < PAIRS:
                            counted(pe, "hf", n * UN0, p - 2 if p >= 2 else p - 3)
                            mm(bank(3 + p % 2), PICKW[:, 2 * p:2 * p + 2, :].rearrange("p e f -> p (e f)"),
                               CWT[:, bass.ds(n * TB, TB)], start=True, stop=True).then_inc(sem["bc"], 1)
                    if p >= LAG:
                        q = p - LAG
                        M = P if q < PAIRS else 64
                        if q % (PAIRS // WCH) == 0:
                            ready(pe, "wd_l", 0, q // (PAIRS // WCH))
                        counted(pe, "lo", n * UN0, q)
                        mm3(bank(5), (WDH[0:M, q, :], WDL[0:M, q, :]), (HH[q % 3][0:M, :], HL[q % 3][0:M, :]),
                            q == 0, q == UN0 - 1).then_inc(sem["down"], 1)
                ready(pe, "yt", n)
                counted(pe, "d_x", n, -1)
                for s in range(4):
                    last = tr(bank(6)[:, P * s:P * s + P], YF[:, P * s:P * s + P], IDN[:])
                last.then_inc(sem["ytp"], 1)

            counted(pe, "d_x", 0, NT - 1)
            ready(pe, "wz_l", 0, 1)
            with pe.Fori(0, B) as b:
                ready(pe, "exn", b)
                for s in range(SB):
                    last = tr(PA[:, P * s:P * s + P], XN1[:, s, :], IDN[:])
                last.then_inc(sem["ext"], 1)
                ready(pe, "exf", b)
                for s in range(SB):
                    last = mm(PD[:, E1 * s:E1 * s + E1], XF1[:, P * s:P * s + P], GW[:], start=True, stop=True)
                last.then_inc(sem["lg"], 1)
                ready(pe, "xfp", b)
                for s in range(SB):
                    last = mm(PC[:, P * s:P * s + P], XFP[:, P * s:P * s + P], WV1[:], start=True, stop=True)
                last.then_inc(sem["vp"], 1)
                pe.wait_ge(sem["extl"], b + 2)
                for h in range(2):
                    t = bass.ds(b * N + TB * h, TB)
                    last = mm3(PB[:, TB * h:TB * h + TB], (WV1H[:], WV1L[:]), (XTH[:, t], XTL[:, t]), True, True)
                last.then_inc(sem["pp"], 1)

            def scores(g, k, par, pair):
                half, kc = k // 8, k % 8
                if kc == 0 and pair == 0:
                    pe.wait_ge(sem["m_r"], g * 32 + 16 * (half + 1))
                counted(pe, "exq", g * 32, 2 * (k - 1) + pair)
                for jj in range(2):
                    last = mm((PA, PB)[pair][:, TB * jj:TB * jj + TB], L[par][0:MR + 2 * HG, 2 * pair + jj, P * kc:P * kc + P],
                              R[par][0:MR + 2 * HG, TB * half:TB * half + TB], start=True, stop=True)
                last.then_inc(sem["sc"], 1)

            def products(g, k, par):
                half, kc = k // 8, k % 8
                if k == 0:
                    ready(pe, "va", g)
                counted(pe, "exq", g * 32, 2 * k + 1)
                if kc == 0:
                    counted(pe, "osb", g * 2, half - 1)
                for j in range(HG):
                    last = mm(bank(7)[32 * j:32 * j + 32, :], VA[par][:, kc, j, :],
                              EX1[(2 * k + j // 2) % 4][:, TB * (j % 2):TB * (j % 2) + TB], start=(kc == 0), stop=(kc == 7))
                last.then_inc(sem["av"], 1)

            def pslot(x, idx, g, par):
                kind, u, ahead = seq_of(idx)
                gp = (par + ahead) % 2
                mb = slot_bank(idx)
                if not (idx[1] == "pro" and idx[0] < 3):
                    counted(pe, "red", x, -3)
                if kind == "max":
                    if u == 0:
                        pe.wait_ge(sem["lr"], (g + ahead) * (15 * 16) + 16 * (2 * HG + 15))
                    c, j, h = u // 8, (u % 8) // 2, u % 2
                    mm(mb, L[gp][0:MR, j, P * c:P * c + P], R[gp][0:MR, TB * h:TB * h + TB],
                       start=True, stop=True).then_inc(sem["mx"], 1)
                else:
                    ready(pe, "neg", (g + ahead) * 2 + u)
                    tr(mb[0:HG * 4, 0:P], MN[gp][:, u, :], IDN[:]).then_inc(sem["mx"], 1)

            def group(g, par, kind):
                n_slots = SLOTS if kind == "body" else SLOTS_END
                for k in range(16):
                    mine = range(min(SLOTS * k // 16, n_slots), min(SLOTS * (k + 1) // 16, n_slots))
                    mid = (mine.start + mine.stop) // 2
                    for pair in range(2):
                        if k < 15:
                            scores(g, k + 1, par, pair)
                        elif kind == "body":
                            scores(g + 1, 0, 1 - par, pair)
                        for idx in (range(mine.start, mid), range(mid, mine.stop))[pair]:
                            pslot(g * SLOTS + (PRO + idx), (idx, kind), g, par)
                    products(g, k, par)

            ready(pe, "ve", 0, B - 1)
            for idx in range(PRO):
                pslot(idx, (idx, "pro"), 0, 0)
            for pair in range(2):
                scores(0, 0, 0, pair)
            with pe.Fori(0, NG // 2 - 1) as i:
                for par in range(2):
                    group(i * 2 + par, par, "body")
            group(NG - 2, 0, "body")
            group(NG - 1, 1, "end")

            ready(pe, "b2_l")
            counted(pe, "osb", 2 * NG - 1)
            with pe.Fori(0, NT) as n:
                u0 = n * U1
                tok = bass.ds(n * TB, TB)
                xh, xl = XTH[:, tok], XTL[:, tok]
                ready(pe, "gss", n)
                counted(pe, "fin", n, -1)
                for s in range(4):
                    last = tr(bank(6)[0:2 * E1, P * s:P * s + P], GSS[:, s, :].bitcast(F32), IDN[:])
                last.then_inc(sem["gstp"], 1)
                for p in range(U1 + LAG):
                    if p < U1:
                        if p % (U1 // WCH) == 0:
                            ready(pe, "w1_l", 0, p // (U1 // WCH))
                        c = slice(P * p, P * p + P)
                        counted(pe, "s1", u0, before(p, 2, U1))
                        mm3(bank(p % 2), (W1H[:, 0, c], W1L[:, 0, c]), (xh, xl), True, True).then_inc(sem["h1"], 1)
                        counted(pe, "ah", u0, before(p, 2, U1))
                        mm3(bank(2 + p % 2), (W1H[:, 1, c], W1L[:, 1, c]), (xh, xl), True, True).then_inc(sem["h0"], 1)
                        if p % 2 == 0:
                            e = p // 2
                            if e == 0:
                                ready(pe, "gt", n)
                            counted(pe, "hf1", u0, 2 * e - 3)
                            mm(bank((4, 7)[e % 2]), PICK8[:, e:e + 1].to_broadcast([2 * E1, P]), GTT[:],
                               start=True, stop=True).then_inc(sem["bg"], 1)
                    if p >= LAG:
                        q = p - LAG
                        if q % (U1 // WCH) == 0:
                            ready(pe, "w2_l", 0, q // (U1 // WCH))
                        counted(pe, "lo1", u0, q)
                        if q == 0:
                            counted(pe, "dn1", u0, -1)
                            ready(pe, "gt", n)
                            mm(bank(5), B2H[:], GTT[:], start=True, stop=False)
                            mm(bank(5), B2L[:], GTT[:], start=False, stop=False)
                        if q == U1 // 2:
                            ready(pe, "on", n, 1)
                            mm(bank(5), WO1[:], ON[:], start=False, stop=False).then_inc(sem["pj"], 1)
                        mm3(bank(5), (W2H[:, q, :], W2L[:, q, :]), (HH1[q % 3][:], HL1[q % 3][:]),
                            False, q == U1 - 1).then_inc(sem["dn1"], 1)
                ready(pe, "y2s", n)
                for s in range(4):
                    last = tr(bank(6)[:, P * s:P * s + P], Y2[:, P * s:P * s + P], IDN[:])
                last.then_inc(sem["ytp2"], 1)


def kernel(**inputs):
    from concourse import bacc as _bacc
    from concourse.bass_utils import run_bass_kernel_spmd as _run

    f = {k: np.ascontiguousarray(v) for k, v in inputs.items()}
    x = f["L0_attn_x"]
    B, N, D = x.shape
    QK, E0, E1 = f["L0_attn_Wqk"].shape[0], f["L0_ffn_W_up"].shape[0], f["L1_ffn_w0"].shape[0]
    H1 = f["L1_ffn_w0"].shape[1]
    heads = f["L0_attn_gamma"].shape[0]
    swap = np.r_[QK // 2:QK, 0:QK // 2]
    wqk, bqk = f["L0_attn_Wqk"], f["L0_attn_bqk"]
    gam, bet = f["L0_attn_gamma"], f["L0_attn_beta"]

    def four(m):
        return np.concatenate([m] * heads, 0)

    bg = f["L0_attn_bg"].reshape(2, P)
    zero = np.zeros(P, np.float32)
    cols0 = np.stack([f["L0_attn_ln1_w"], f["L0_attn_ln1_b"], four(bqk), four(bqk[swap]), gam.reshape(-1),
                      bet.reshape(-1), gam[:, swap].reshape(-1), bet[:, swap].reshape(-1), bg[0], bg[1]]
                     + [zero] * 6, 1)
    halves0 = f["L1_ffn_b0"].reshape(-1, P)
    halves1 = f["L1_ffn_b1"].reshape(-1, P)
    cols1 = np.concatenate([f["L1_attn_bv"][:, None], f["L1_attn_bo"][:, None], halves0.T, halves1.T], 1)
    data = {
        "x": x,
        "wz": np.concatenate([four(wqk).T, four(wqk[swap]).T, f["L0_attn_Wv"].T, f["L0_attn_Wg"].T], 1),
        "cols0": cols0, "cols1": cols1,
        "bv0": f["L0_attn_bv"][None], "bo0": f["L0_attn_bo"][None], "wo0": f["L0_attn_Wo"].T,
        "ln2_w": f["L0_attn_ln2_w"][None], "ln2_b": f["L0_attn_ln2_b"][None], "pos_emb": f["L0_attn_pos_emb"][None, :33],
        "centroids": f["L0_ffn_centroids"].T, "expert_biases": f["L0_ffn_expert_biases"][None],
        "w_up": np.concatenate([f["L0_ffn_W_up"].transpose(1, 0, 2).reshape(D, -1), f["L0_ffn_Ws_up"]], 1),
        "w_down": f["L0_ffn_W_down"].reshape(-1, D), "ws_down": f["L0_ffn_Ws_down"],
        "wv1": f["L1_attn_Wv"].T, "bv1": f["L1_attn_bv"][None], "wo1": f["L1_attn_Wo"].T,
        "gate_w": f["L1_ffn_gate_w"].T, "gate_b": f["L1_ffn_gate_b"][None],
        "w0": f["L1_ffn_w0"].transpose(2, 0, 1).reshape(D, -1), "w1": f["L1_ffn_w1"].transpose(2, 0, 1).reshape(D, -1),
        "w2": f["L1_ffn_w2"].transpose(0, 2, 1).reshape(E1 * H1, D),
        "b2": np.concatenate([f["L1_ffn_b2"]] * 2, 0),
    }
    data.update(shape_constants(N, QK, 64, 32))
    nc = _bacc.Bacc("TRN2", target_bir_lowering=False, num_devices=1)
    arrays, a = {}, {}
    for name, v in data.items():
        arrays["in_" + name] = np.ascontiguousarray(v)
        a[name] = nc.dram_tensor("in_" + name, v.shape, mybir.dt.from_np(v.dtype), kind="ExternalInput").ap()
    out = nc.dram_tensor("out_x", (B * N, D), F32, kind="ExternalOutput").ap()
    build_program(nc, a, out)
    r = _run(nc, [arrays], core_ids=[0])
    return r.results[0]["out_x"].reshape(B, N, D)
```

```python
from contextlib import ExitStack

import numpy as np

import concourse.bass as bass
from concourse import mybir

ALU = mybir.AluOpType
ACT = mybir.ActivationFunctionType
AX = mybir.AxisListType
F32 = mybir.dt.float32
R32 = mybir.dt.float32r

P = 128
EPS = 1e-5
LOWEST = -3.0e38
CREDIT = 4


def shape_constants(N, QK):
    half = QK // 2
    pos = np.arange(N, dtype=np.float32)
    inv = (np.float32(10000.0) ** (-np.arange(half, dtype=np.float32) / np.float32(half))).astype(np.float32)
    ang = (pos[:, None] * inv[None, :]).astype(np.float32)
    sin, cos = np.sin(ang).astype(np.float32), np.cos(ang).astype(np.float32)
    heads = P // QK
    cos_t = np.tile(np.concatenate([cos, cos], 1).T, (heads, 1))
    sin_t = np.tile(np.concatenate([-sin, sin], 1).T, (heads, 1))
    k = np.arange(P)
    return {
        "c_cos": cos_t.astype(np.float32),
        "c_sin": sin_t.astype(np.float32),
        "c_ident": np.eye(P, dtype=np.float32),
        "c_pick64": (k[:, None] % 64 == np.arange(64)[None, :]).astype(np.float32),
        "c_pick8": (np.arange(16)[:, None] % 8 == np.arange(8)[None, :]).astype(np.float32),
    }


def build_program(nc, a, out):
    B, N, D = a["x"].shape
    T = B * N
    SUB = T // P
    SB = N // P
    TB = 512
    NT = T // TB
    GROUP = 64
    E0 = a["centroids"].shape[1]
    PAIRS = E0 // 2
    assert (PAIRS + 1) % 3 == 0
    UN0 = PAIRS + 1
    E1 = a["gate_w"].shape[1]
    HV = a["bv0"].shape[1]
    H1 = HV // P
    U1 = 2 * E1
    HG = 4
    DK = 8
    NG = B * HG
    LAG, LAG1 = 3, 4
    TURN, TURN1 = LAG + 2, LAG1 + 2
    PROJECT_AT = 11
    assert 2 * E1 % 4 == 0
    WCH = 4
    MAXIMA = 2 * 4 * HG * (N // TB)
    CARRY = 16
    SLOTS, T1, T0 = MAXIMA + 2, CARRY + 3, CARRY + 36
    PRO, PRO_T0 = MAXIMA - CARRY + 1, 38
    SLOTS_END = CARRY + 1
    OD_W = ("od_half0", "od_half1")
    MR = 3 * HG * DK
    AV0 = 17
    NI = N // 16
    SCALE = 1.0 / float(DK) ** 0.5

    ctx = ExitStack()
    with ctx:
        names = """
        passed rec den_in rd_w x_rest p_in pickw od_half0 od_half1 ot_in xfp w_in c_in x_in qqd ph_w lr m_w m_r out_s w2_in  wz_h wz_l x_var x_std xn z_var
        z_std z xt xf xth xtl zt zf zth ztl aff sig bi cs cst cwt qp qs qa qb qr v1p v2p vb1 vb2 v1
        v2 g0p g1p g0 g1 lkt lk kvp kv st tb att ot0 ot1 og0 og1 yp y y_var y_std yn yw yb xr wu_h
        wu_l wd_h wd_l up bc silu hf hi lo down yt ytp d_x e_var e_std exn ext exf exth extl lg
        shift ex gs gt pp pf ph pl vp ve va sc exq av osb mx red neg mhi l_zero gss gstp pj w1_h
        w1_l w2_h w2_l b2_h b2_l h1 h0 bg s1 ah hf1 hi1 lo1 dn1 on y2s ytp2 fin route rope
        route2 x_own z_own y_own e_own
        """.split()
        sem = {n: ctx.enter_context(nc.semaphore("s_" + n)) for n in names}

        base = (nc.sbuf_base + 63) // 64 * 64
        KB = 1024
        place = {}

        def region(name, start, size):
            place[name] = [base + start, base + start + size]

        def sb(where, name, shape, dt=F32):
            at, end = place[where]
            size = 4 * int(np.prod(shape[1:]))
            size = (size + 31) // 32 * 32
            assert at + size <= end, (where, name, at + size - end)
            place[where][0] = at + size
            return nc.alloc_sbuf_tensor_at(name, shape, dt, offset=at)

        region("keep", 0, 54 * KB)
        region("ffn0_lo", 54 * KB, 33 * KB)
        region("ffn0_hi", 87 * KB, 33 * KB)
        region("gates", 120 * KB, 16 * KB)
        region("work", 136 * KB, 71 * KB + 512)
        region("attn0", 87 * KB, 33 * KB)
        region("attn0w", 120 * KB + 16 * KB, 71 * KB + 512)
        region("attn1b", 54 * KB, 48 * KB)
        region("ffn1c", 102 * KB, 2 * KB)
        region("gates1", 104 * KB, 16 * KB)
        region("v_all", 120 * KB, 16 * KB)
        region("ffn1_lo", 136 * KB, 24 * KB)
        region("attn1", 184 * KB, 15 * KB)
        region("attn1r", 199 * KB, 8 * KB + 512)
        region("ffn1_hi", 160 * KB, 24 * KB)
        region("ffn1w", 184 * KB, 23 * KB + 512)
        region("ffn1v", 120 * KB, 16 * KB)
        region("ffn1x", 54 * KB, 48 * KB)
        region("prep1", 160 * KB, 27 * KB)
        region("prep1w", 187 * KB, 3 * KB + 512)

        X = sb("keep", "X", [P, SUB, D])
        XTH = sb("keep", "XTH", [P, T], R32)
        XTL = sb("keep", "XTL", [P, T], R32)
        IDN = sb("keep", "IDN", [P, P])
        PICK64 = sb("keep", "PICK64", [P, 64], R32)
        PICK8 = sb("keep", "PICK8", [16, 8], R32)
        COLS = sb("keep", "COLS", [P, 16])
        COL1 = sb("keep", "COL1", [P, 2 + 2 * U1])
        ST = sb("keep", "ST", [P, SB, 6])
        MV = sb("keep", "MV", [P, SB, 2])
        VE = sb("keep", "VE", [P, SB])
        SD = sb("keep", "SD", [P, SB])
        RS = sb("keep", "RS", [P, SB])
        STAGE = sb("keep", "STAGE", [P, 64 + 8])

        WUL_RAW = nc.alloc_sbuf_tensor_at("WUL_RAW", [P, E0 * 64 + 64], F32, offset=place["ffn0_lo"][0])
        WUL = sb("ffn0_lo", "WUL", [P, E0 * 64 + 64], R32)
        WDL_RAW = nc.alloc_sbuf_tensor_at("WDL_RAW", [P, UN0, D], F32, offset=place["ffn0_lo"][0])
        WDL = sb("ffn0_lo", "WDL", [P, UN0, D], R32)
        WUH = sb("ffn0_hi", "WUH", [P, E0 * 64 + 64], R32)
        WDH = sb("ffn0_hi", "WDH", [P, UN0, D], R32)
        CWT = sb("gates", "CWT", [P, T], R32)
        SU = [sb("work", f"SU{i}", [P, TB]) for i in range(2)]
        HF = [sb("work", f"HF{i}", [P, TB]) for i in range(3)]
        HH = [sb("work", f"HH{i}", [P, TB], R32) for i in range(3)]
        HL = [sb("work", f"HL{i}", [P, TB], R32) for i in range(3)]
        YF = sb("work", "YF", [P, TB])
        PICKW = sb("work", "PICKW", [P, E0, 64], R32)

        XN = sb("attn0", "XN", [P, SB, D])
        Z = sb("attn0", "Z", [P, SB, D])
        XF = sb("attn0", "XF", [P, N])
        ZF = sb("attn0", "ZF", [P, N])
        ZTH = sb("attn0", "ZTH", [P, N], R32)
        ZTL = sb("attn0", "ZTL", [P, N], R32)
        V = sb("attn0", "V", [P, SB, HV])
        w = "attn0w"
        WZR = nc.alloc_sbuf_tensor_at("WZR", [P, 2 * P + 2 * HV], F32, offset=place[w][0])
        WZL = sb(w, "WZL", [P, 2 * P + 2 * HV], R32)
        WZH = sb(w, "WZH", [P, 2 * P + 2 * HV], R32)
        WO0 = sb(w, "WO0", [P, H1, D])
        CEN = sb(w, "CEN", [P, E0])
        COS = sb(w, "COS", [P, N])
        SIN = sb(w, "SIN", [P, N])
        BVB = sb(w, "BVB", [P, HV])
        BOB = sb(w, "BOB", [P, D])
        L2W = sb(w, "L2W", [P, D])
        L2B = sb(w, "L2B", [P, D])
        EBB = sb(w, "EBB", [P, E0])
        BIAS = sb(w, "BIAS", [P, GROUP])
        SIG = sb(w, "SIG", [P, SB, E0])
        BI = sb(w, "BI", [P, SB, E0])
        CUT = sb(w, "CUT", [P, SB, E0])
        CS = sb(w, "CS", [P, SB, 2 * E0], R32)
        TOP8 = sb(w, "TOP8", [P, SB, 8])
        WS = sb(w, "WS", [P, 3, SB])
        QA = sb(w, "QA", [P, N])
        QB = sb(w, "QB", [P, N])
        G = sb(w, "G", [P, H1, N])
        AT = sb(w, "AT", [P, SB, P])
        TMP = sb(w, "TMP", [P, SB, GROUP])
        LK = sb(w, "LK", [P, SB, 32])
        KV = sb(w, "KV", [P, HV])
        QQ = sb(w, "QQ", [P, N])
        OG = sb(w, "OG", [P, H1, N])
        YT = sb(w, "YT", [P, SB, D])

        XN1 = sb("prep1", "XN1", [P, SB, D])
        XF1 = sb("prep1", "XF1", [P, N])
        XFP = sb("prep1", "XFP", [P, N])
        PF = sb("prep1", "PF", [P, N])
        PH = sb("prep1", "PH", [P, N], R32)
        PL = sb("prep1", "PL", [P, N], R32)
        WV1H = sb("prep1w", "WV1H", [P, D], R32)
        WV1L = sb("prep1w", "WV1L", [P, D], R32)
        WV1 = sb("prep1w", "WV1", [P, D])
        GW = sb("prep1w", "GW", [P, E1])
        GBB = sb("prep1w", "GBB", [P, E1])
        BVB1 = sb("prep1w", "BVB1", [P, D])
        LG = sb("prep1", "LG", [P, SB, 16])
        TOP2 = sb("prep1", "TOP2", [P, SB, 8])
        SEL2 = sb("prep1", "SEL2", [P, SB, 8])
        CUT2 = sb("prep1", "CUT2", [P, SB, 16])
        MASK2 = sb("prep1", "MASK2", [P, SB, E1])
        SH = sb("prep1", "SH", [P, SB, E1])
        EX = sb("prep1", "EX", [P, SB, E1])
        GM = sb("prep1", "GM", [P, SB, E1])
        GSUM = sb("prep1", "GSUM", [P, 2, SB])
        GATE = sb("prep1", "GATE", [P, SB, E1])
        GS = sb("keep", "GS", [P, SUB, 2 * E1], R32)
        V1 = sb("v_all", "V1", [P, NG, SB, HG, DK])
        L = [sb("attn1b", f"L{i}", [P, HG, N], R32) for i in range(2)]
        R = [sb("attn1r", f"R{i}", [P, N], R32) for i in range(2)]
        EX1 = [sb("attn1b", f"EX1{i}", [P, 2 * TB]) for i in range(4)]
        VA = [sb("attn1", f"VA{i}", [P, SB, HG, 32]) for i in range(2)]
        OSB = [sb("attn1", f"OSB{i}", [P, TB]) for i in range(2)]
        MX = [sb("attn1", f"MX{i}", [P, 2, HG, 4, 2]) for i in range(2)]
        MN = [sb("attn1", f"MN{i}", [P, 2, HG * 4]) for i in range(2)]
        MH = [sb("attn1", f"MH{i}", [HG * 4, P], R32) for i in range(2)]
        ML = [sb("attn1", f"ML{i}", [HG * 4, P], R32) for i in range(2)]
        ONE = nc.alloc_sbuf_tensor_at("ONE", [P, N], R32, offset=base + 54 * KB + 32 * KB)
        F1 = E1 * 2 * P
        W1R = nc.alloc_sbuf_tensor_at("W1R", [P, 2, F1], F32, offset=place["ffn1_lo"][0])
        W1L = sb("ffn1_lo", "W1L", [P, 2, F1], R32)
        W2R = nc.alloc_sbuf_tensor_at("W2R", [P, U1, D], F32, offset=place["ffn1_lo"][0])
        W2L = sb("ffn1_lo", "W2L", [P, U1, D], R32)
        W1H = sb("ffn1_hi", "W1H", [P, 2, F1], R32)
        W2H = sb("ffn1_hi", "W2H", [P, U1, D], R32)
        WO1 = sb("ffn1c", "WO1", [P, D])
        OT = sb("ffn1v", "OT", [P, 2 * HG, NI])
        REC = sb("ffn1x", "REC", [P, 2 * HG, NI])
        DEN = sb("ffn1x", "DEN", [P, NI])
        RD = sb("ffn1x", "RD", [P, NI])
        B2R = sb("ffn1c", "B2R", [16, D])
        B2H = sb("ffn1c", "B2H", [16, D], R32)
        B2L = sb("ffn1c", "B2L", [16, D], R32)
        S1 = [sb("ffn1w", f"S1{i}", [P, TB]) for i in range(2)]
        AH = [sb("ffn1w", f"AH{i}", [P, TB]) for i in range(2)]
        HH1 = [sb("ffn1v", f"HH1{i}", [P, TB], R32) for i in range(4)]
        HL1 = [sb("ffn1x", f"HL1{i}", [P, TB], R32) for i in range(4)]
        GTT = sb("gates1", "GTT", [16, T], R32)
        ON = sb("ffn1w", "ON", [P, TB])
        Y2 = sb("ffn1w", "Y2", [P, TB])
        HF1 = [sb("ffn1w", f"HF1{i}", [P, TB]) for i in range(2)]
        FIN = sb("ffn1x", "FIN", [P, 4, D])

        phd = nc.dram_tensor("phd", [NG * 32, N], F32)
        pld = nc.dram_tensor("pld", [NG * 32, N], F32)
        od = nc.dram_tensor("od", [NG * HG, 32, N], F32)
        rd = nc.dram_tensor("rd", [NG * HG, 16, NI], F32)
        md = [nc.dram_tensor(f"md{i}", [2, 2, HG, TB], F32) for i in range(2)]

        PA, PB, PC, PD = [ctx.enter_context(nc.psum_tensor(n, [P, 2 * TB], F32)) for n in ("PA", "PB", "PC", "PD")]

        def bank(i):
            t = (PA, PB, PC, PD)[i // 2]
            return t[:, TB * (i % 2):TB * (i % 2) + TB]

        block = ctx.enter_context(nc.Block())

        def before(p, k, units):
            return p - k if p >= k else max(u for u in range(units) if u % k == p) - units

        def wu_cols(c):
            w = PAIRS // WCH * P
            return slice(w * c, w * c + w + (64 if c == WCH - 1 else 0))

        def wd_units(c):
            return slice(PAIRS // WCH * c, PAIRS // WCH * (c + 1))

        def seq_of(at):
            idx, kind = at
            if kind == "pro":
                return ("turn", 0, 0) if idx == PRO_T0 else ("max", idx - (idx > PRO_T0), 0)
            if idx < CARRY:
                return "max", MAXIMA - CARRY + idx, 0
            if kind == "end" or idx == T1:
                return "turn", 1, 0
            if idx == T0:
                return "turn", 0, 1
            return "max", idx - CARRY - (idx > T1) - (idx > T0), 1

        def slot_bank(at):
            return bank(4 + (at[0] + (0 if at[1] == "pro" else PRO)) % 3)

        def nth(n=0, c=0):
            return n + (c + 1)

        def nth_free(n, c=0):
            return n + (c + 1 + CREDIT)

        def mm3(out, w, x, start, stop):
            nc.tensor.matmul(out, w[0], x[0], start=start, stop=False)
            nc.tensor.matmul(out, w[0], x[1], start=False, stop=False)
            return nc.tensor.matmul(out, w[1], x[0], start=False, stop=stop)

        consts = (
            (IDN[:], a["c_ident"]), (COLS[:], a["cols0"]), (WZR[:], a["wz"]), (CEN[:], a["centroids"]),
            (EBB[:], a["expert_biases"].partition_broadcast(P)),
            (BIAS[:], a["bias"]),
            (COS[:], a["c_cos"]), (SIN[:], a["c_sin"]), (STAGE[:, 0:64], a["c_pick64"]),
            (STAGE[0:16, 64:72], a["c_pick8"]), (BVB[:], a["bv0"].partition_broadcast(P)),
            (BOB[:], a["bo0"].partition_broadcast(P)), (L2W[:], a["ln2_w"].partition_broadcast(P)),
            (L2B[:], a["ln2_b"].partition_broadcast(P)), (WO0[:], a["wo0"].rearrange("(h p) d -> p h d", p=P)),
            (COL1[:], a["cols1"]),
        )

        @block.sync
        def _(sp):
            sp.sem_inc(sem["ph_w"], 16)
            sp.sem_inc(sem["m_w"], 64)
            sp.sem_inc(sem["out_s"], 16)
            sp.sem_inc(sem["rd_w"], 16)
            for name in OD_W:
                sp.sem_inc(sem[name], 16)
            for b in range(B):
                sp.dma_start(X[:, SB * b:SB * b + SB, :],
                             a["x"][b].rearrange("(s p) d -> p s d", p=P)).then_inc(sem["x_in" if b == 0 else "x_rest"], 16)
                if b == 0:
                    for dst, src in consts:
                        sp.dma_start(dst, src).then_inc(sem["c_in"], 16)
            sp.dma_start(WUL_RAW[:], a["w_up"]).then_inc(sem["w_in"], 16)
            sp.dma_start(WDL_RAW[:, 0:PAIRS, :], a["w_down"].rearrange("(u p) d -> p u d", p=P)).then_inc(sem["w_in"], 16)
            sp.dma_start(WDL_RAW[0:64, PAIRS, :], a["ws_down"]).then_inc(sem["w_in"], 16)
            with sp.Fori(0, B) as b:
                sp.wait_ge(sem["qr"], nth(b))
                sp.dma_start(QQ[64:96, :], QA[0:32, :]).then_inc(sem["qqd"], 16)
            sp.wait_ge(sem["xr"], B + 1)
            sp.dma_start(WV1[:], a["wv1"]).then_inc(sem["p_in"], 16)
            sp.dma_start(GW[:], a["gate_w"]).then_inc(sem["p_in"], 16)
            sp.dma_start(GBB[:], a["gate_b"].partition_broadcast(P)).then_inc(sem["p_in"], 16)
            sp.dma_start(BVB1[:], a["bv1"].partition_broadcast(P)).then_inc(sem["p_in"], 16)
            sp.wait_ge(sem["d_x"], nth_free(0, NT - 1))
            sp.dma_start(W1R[:, 0, :], a["w1"]).then_inc(sem["w2_in"], 16)
            sp.dma_start(W1R[:, 1, :], a["w0"]).then_inc(sem["w2_in"], 16)
            sp.dma_start(W2R[:], a["w2"].rearrange("(u p) d -> p u d", p=P)).then_inc(sem["w2_in"], 16)
            sp.dma_start(WO1[:], a["wo1"]).then_inc(sem["w2_in"], 16)
            sp.dma_start(B2R[:], a["b2"]).then_inc(sem["w2_in"], 16)
            sp.wait_ge(sem["l_zero"], nth(0, 2))
            for par in range(2):
                for j in range(HG):
                    sp.dma_start(L[par][MR + j:MR + 2 * HG:HG, j, :].bitcast(F32), ONE[0:2, :].bitcast(F32)).then_inc(sem["lr"], 16)

            def load_lr(g, par):
                for r, (l, q) in enumerate(((phd, phd), (phd, pld), (pld, phd))):
                    sp.dma_start(R[par][HG * DK * r:HG * DK * (r + 1), :].bitcast(F32),
                                 q[bass.ds(g * 32, 32), :]).then_inc(sem["lr"], 16)
                    for j in range(HG):
                        rows = slice(HG * DK * r + DK * j, HG * DK * r + DK * j + DK)
                        sp.dma_start(L[par][rows, j, :].bitcast(F32), l[bass.ds(g * 32 + j * DK, DK), :]).then_inc(sem["lr"], 16)

            def store_halves(b):
                sp.wait_ge(sem["pl"], nth(b))
                sp.dma_start(phd[bass.ds(b * P, P), :], PH[:].bitcast(F32)).then_inc(sem["ph_w"], 16)
                sp.dma_start(pld[bass.ds(b * P, P), :], PL[:].bitcast(F32)).then_inc(sem["ph_w"], 16)

            store_halves(0)
            sp.wait_ge(sem["ph_w"], 32 + 16)
            load_lr(0, 0)
            with sp.Fori(0, B - 1) as i:
                store_halves(i + 1)
            sp.wait_ge(sem["ph_w"], 32 * B + 16)
            sp.wait_ge(sem["gs"], nth(0, B - 1))

            def maxima(g, half, par, slot):
                e = 2 * g + half
                sp.wait_ge(sem["red"], nth_free(slot))
                sp.dma_start(md[half][par, 0].rearrange("j (c q) -> (j c) q", q=P), MH[half][:].bitcast(F32)).then_inc(sem["m_w"], 16)
                sp.dma_start(md[half][par, 1].rearrange("j (c q) -> (j c) q", q=P), ML[half][:].bitcast(F32)).then_inc(sem["m_w"], 16)
                sp.wait_ge(sem["m_w"], e * 32 + 96)
                sp.dma_start(R[par][MR:MR + 2 * HG, TB * half:TB * half + TB].bitcast(F32),
                             md[half][par].rearrange("x j q -> (x j) q")).then_inc(sem["m_r"], 16)

            def store_out(g, half):
                sp.wait_ge(sem["osb"], nth_free(g * 2, half))
                sp.dma_start(od[bass.ds(g * HG, HG), :, TB * half:TB * half + TB].rearrange("h r q -> (h r) q"),
                             OSB[half][:]).then_inc(sem[OD_W[half]], 16)

            maxima(0, 0, 0, PRO_T0)
            with sp.Fori(0, NG // 2 - 1) as i:
                for par in range(2):
                    sp.wait_ge(sem["av"], (i * 2 + par) * 16 + AV0)
                    load_lr(i * 2 + (par + 1), 1 - par)
                    maxima(i * 2 + par, 1, par, (i * 2 + par) * SLOTS + (PRO + T1))
                    store_out(i * 2 + par, 0)
                    maxima(i * 2 + (par + 1), 0, 1 - par, (i * 2 + par) * SLOTS + (PRO + T0))
                    store_out(i * 2 + par, 1)
            sp.wait_ge(sem["av"], (NG - 2) * 16 + AV0)
            load_lr(NG - 1, 1)
            maxima(NG - 2, 1, 0, (NG - 2) * SLOTS + PRO + T1)
            store_out(NG - 2, 0)
            maxima(NG - 1, 0, 1, (NG - 2) * SLOTS + PRO + T0)
            store_out(NG - 2, 1)
            maxima(NG - 1, 1, 1, (NG - 1) * SLOTS + PRO + CARRY)
            for half in range(2):
                store_out(NG - 1, half)
            for name in OD_W:
                sp.wait_ge(sem[name], NG * 16 + 16)

            def load_heads(n):
                heads = bass.ds(n * (2 * HG), 2 * HG)
                sp.dma_start(DEN[:], od[heads, DK, :].rearrange("h (c i) -> h c i", i=NI)).then_inc(sem["den_in"], 16)
                sp.wait_ge(sem["on"], n + 1)
                sp.sem_inc(sem["passed"], 1)
                for h in range(2 * HG):
                    sp.dma_start(OT[:, h, :], od[bass.ds(n * (2 * HG) + h, 1), 0:DK, :].rearrange(
                        "h d (c i) -> c (h d) i", i=NI)).then_inc(sem["ot_in"], 16)
                sp.wait_ge(sem["rec"], nth(n))
                sp.dma_start(rd[heads].rearrange("h c i -> (h c) i"), RD[:]).then_inc(sem["rd_w"], 16)
                sp.wait_ge(sem["rd_w"], n * 16 + 32)
                for h in range(2 * HG):
                    sp.dma_start(REC[:, h, :], rd[bass.ds(n * (2 * HG) + h, 1)].rearrange("h c i -> (h c) i").unsqueeze(1)
                                 .to_broadcast([16, DK, NI])).then_inc(sem["ot_in"], 16)

            def store_tile(n):
                sp.wait_ge(sem["fin"], nth_free(n))
                sp.dma_start(out[bass.ds(n * TB, TB), :].rearrange("(s p) d -> p s d", p=P), FIN[:]).then_inc(sem["out_s"], 16)

            load_heads(0)
            with sp.Fori(0, NT - 1) as i:
                load_heads(i + 1)
                store_tile(i)
            store_tile(NT - 1)
            sp.wait_ge(sem["out_s"], 16 * (NT + 1))

        def scale_shift_add(e, b):
            e.wait_ge(sem["yn"], nth(b))
            e.tensor_tensor(YT[:], YT[:], L2W[:].unsqueeze(1).to_broadcast([P, SB, D]), ALU.mult).then_inc(sem["yw"], 1)
            e.wait_ge(sem["yw"], nth(b))
            e.tensor_tensor(YT[:], YT[:], L2B[:].unsqueeze(1).to_broadcast([P, SB, D]), ALU.add).then_inc(sem["yb"], 1)
            e.wait_ge(sem["yb"], nth(b))
            e.tensor_tensor(X[:, bass.ds(b * SB, SB), :], X[:, bass.ds(b * SB, SB), :], YT[:], ALU.add).then_inc(sem["xr"], 1)

        @block.gpsimd
        def _(pool):
            for name in ("xtl", "extl", "on", "xr"):
                pool.sem_inc(sem[name], 1)
            def split_x(b):
                pool.wait_ge(sem["xf"], nth(b))
                pool.tensor_copy(XTH[:, bass.ds(b * N, N)], XF[:]).then_inc(sem["xth"], 1)
                pool.wait_ge(sem["xth"], nth(b))
                pool.tensor_tensor(XTL[:, bass.ds(b * N, N)], XF[:], XTH[:, bass.ds(b * N, N)], ALU.subtract).then_inc(sem["xtl"], 1)

            with pool.Fori(0, B - 1) as b:
                split_x(b)
                scale_shift_add(pool, b)
            split_x(B - 1)
            pool.wait_ge(sem["og1"], nth(0, B - 1))
            pool.wait_ge(sem["cst"], nth(0, B - 1))
            pool.wait_ge(sem["ot1"], nth(0, B - 1))
            for c in range(WCH):
                es = slice(E0 // WCH * c, E0 // WCH * (c + 1))
                pool.tensor_copy(PICKW[:, es, :], PICK64[:, es].unsqueeze(2).to_broadcast([P, E0 // WCH, 64])
                                 ).then_inc(sem["pickw"], 1)
            pool.wait_ge(sem["d_x"], nth_free(0, NT - 1))
            for t, v in ((L[0], 0.0), (L[1], 0.0), (ONE, 1.0)):
                pool.memset(t[:].bitcast(F32), v).then_inc(sem["l_zero"], 1)
            with pool.Fori(0, B) as b:
                pool.wait_ge(sem["exf"], nth(b))
                pool.tensor_copy(XTH[:, bass.ds(b * N, N)], XF1[:]).then_inc(sem["exth"], 1)
                pool.wait_ge(sem["exth"], nth(b))
                pool.tensor_tensor(XTL[:, bass.ds(b * N, N)], XF1[:], XTH[:, bass.ds(b * N, N)], ALU.subtract).then_inc(sem["extl"], 1)
            pool.wait_ge(sem["pl"], nth(0, B - 1))
            pool.wait_ge(sem["ph_w"], 32 * B + 16)
            pool.wait_ge(sem["gs"], nth(0, B - 1))
            for t in VA:
                pool.memset(t[:], 1.0).then_inc(sem["l_zero"], 1)
            pool.wait_ge(sem["l_zero"], nth(0, 4))

            def value_columns(g, par):
                pool.wait_ge(sem["av"], g * 16 + (AV0 - 16))
                pool.tensor_copy(VA[par][:, :, :, 0:DK],
                                 V1[:, bass.ds(g, 1), :, :, :].rearrange("p g s j d -> p (g s) j d")).then_inc(sem["va"], 1)

            value_columns(0, 0)
            pool.wait_ge(sem["w2_in"], 16 * 5)
            for raw, high, low in ((W1R, W1H, W1L), (W2R, W2H, W2L), (B2R, B2H, B2L)):
                pool.tensor_copy(high[:], raw[:]).then_inc(sem["w1_h"], 1)
            for c, (raw, high, low) in enumerate(((W1R, W1H, W1L), (W2R, W2H, W2L), (B2R, B2H, B2L))):
                pool.wait_ge(sem["w1_h"], nth(0, c))
                pool.tensor_tensor(low[:], raw[:], high[:], ALU.subtract).then_inc(sem["w1_l"], 1)
            with pool.Fori(0, NG // 2 - 1) as i:
                for par in range(2):
                    value_columns(i * 2 + (par + 1), 1 - par)
            value_columns(NG - 1, 1)
            with pool.Fori(0, NT) as n:
                pool.wait_ge(sem["pj"], n + 1)
                pool.wait_ge(sem["ot_in"], n * (4 * HG * 16) + 4 * HG * 16)
                pool.tensor_tensor(ON[:], OT[:].rearrange("p h i -> p (h i)"), REC[:].rearrange("p h i -> p (h i)"),
                                   ALU.mult).then_inc(sem["on"], 1)

        def norm_stats(e, pre, x_of, n):
            for s in range(SB):
                last = nc.vector.bn_stats(ST[:, s, :], x_of(s))
            last.then_inc(sem[pre + "_own"], 1)
            e.wait_ge(sem[pre + "_own"], nth(n * 3, 0))
            e.sem_inc(sem["passed"], 1)
            for s in range(SB):
                last = nc.vector.bn_aggr(MV[:, s, :], ST[:, s, :])
            last.then_inc(sem[pre + "_own"], 1)
            e.wait_ge(sem[pre + "_own"], nth(n * 3, 1))
            nc.vector.tensor_scalar(VE[:], MV[:, :, 1], EPS, None, ALU.add).then_inc(sem[pre + "_var"], 1)

        def norm_apply(e, pre, x_of, out_of, done, n):
            e.wait_ge(sem[pre + "_std"], nth(n))
            nc.vector.reciprocal(RS[:], SD[:]).then_inc(sem[pre + "_own"], 1)
            e.wait_ge(sem[pre + "_own"], nth(n * 3, 2))
            for s in range(SB):
                last = nc.vector.tensor_scalar(out_of(s), x_of(s), MV[:, s, 0:1], RS[:, s:s + 1],
                                               ALU.subtract, ALU.mult)
            last.then_inc(sem[done], 1)

        def x_sub(b, s):
            return X[:, bass.ds(b * SB + s, 1), :].rearrange("p s d -> p (s d)")

        @block.vector
        def _(dve):
            for name in ("hf", "lo", "d_x", "red", "ah", "hf1", "lo1", "fin"):
                dve.sem_inc(sem[name], CREDIT)
            tt, ts, cp = nc.vector.tensor_tensor, nc.vector.tensor_scalar, nc.vector.tensor_copy
            def weights_low(c):
                dve.wait_ge(sem["wu_h"], nth(0, c))
                tt(WUL[:, wu_cols(c)], WUL_RAW[:, wu_cols(c)], WUH[:, wu_cols(c)], ALU.subtract).then_inc(sem["wu_l"], 1)
                dve.wait_ge(sem["wd_h"], nth(0, c))
                tt(WDL[:, wd_units(c), :], WDL_RAW[:, wd_units(c), :], WDH[:, wd_units(c), :],
                   ALU.subtract).then_inc(sem["wd_l"], 1)
                if c == WCH - 1:
                    dve.wait_ge(sem["wd_h"], nth(0, WCH))
                    tt(WDL[0:64, PAIRS, :], WDL_RAW[0:64, PAIRS, :], WDH[0:64, PAIRS, :], ALU.subtract).then_inc(sem["wd_l"], 1)

            def x_stats(b):
                norm_stats(dve, "x", lambda s: x_sub(b, s), b)

            def x_apply(b):
                norm_apply(dve, "x", lambda s: x_sub(b, s), lambda s: XN[:, s, :], "xn", b)

            def z_stats(b):
                dve.wait_ge(sem["xn"], nth(b))
                norm_stats(dve, "z", lambda s: XN[:, s, :], b)

            def z_apply(b):
                norm_apply(dve, "z", lambda s: XN[:, s, :], lambda s: Z[:, s, :], "z", b)

            def turned_z(b):
                dve.wait_ge(sem["zt"], nth(b))
                ts(ZF[:], PB[:], COLS[:, 0:1], COLS[:, 1:2], ALU.mult, ALU.add).then_inc(sem["zf"], 1)

            def low_z_and_bias(b):
                dve.wait_ge(sem["zth"], nth(b))
                tt(ZTL[:], ZF[:], ZTH[:], ALU.subtract).then_inc(sem["ztl"], 1)
                dve.wait_ge(sem["sig"], nth(b))
                tt(BI[:], PC[:, 0:SB * E0].rearrange("p (s e) -> p s e", e=E0),
                   EBB[:].unsqueeze(1).to_broadcast([P, SB, E0]), ALU.add).then_inc(sem["bi"], 1)

            def batch(b, more):
                dve.wait_ge(sem["qa"], nth(b))
                ts(QA[:], QA[:], COLS[:, 4:5], COLS[:, 5:6], ALU.mult, ALU.add).then_inc(sem["rope"], 1)
                dve.wait_ge(sem["qb"], nth(b))
                ts(QB[:], QB[:], COLS[:, 6:7], COLS[:, 7:8], ALU.mult, ALU.add).then_inc(sem["rope"], 1)
                dve.wait_ge(sem["rope"], nth(b * 4, 0))
                tt(QA[:], QA[:], COS[:], ALU.mult).then_inc(sem["rope"], 1)
                dve.wait_ge(sem["rope"], nth(b * 4, 1))
                tt(QB[:], QB[:], SIN[:], ALU.mult).then_inc(sem["rope"], 1)
                dve.wait_ge(sem["rope"], nth(b * 4, 2))
                dve.wait_ge(sem["rope"], nth(b * 4, 3))
                tt(QA[:], QA[:], QB[:], ALU.add).then_inc(sem["qr"], 1)
                dve.wait_ge(sem["v1p"], nth(b))
                tt(V[:, 0:4, :], PD[:].rearrange("p (s e) -> p s e", e=HV),
                   BVB[:].unsqueeze(1).to_broadcast([P, 4, HV]), ALU.add).then_inc(sem["vb1"], 1)
                dve.wait_ge(sem["v2p"], nth(b))
                tt(V[:, 4:8, :], PA[:].rearrange("p (s e) -> p s e", e=HV),
                   BVB[:].unsqueeze(1).to_broadcast([P, 4, HV]), ALU.add).then_inc(sem["vb2"], 1)
                dve.wait_ge(sem["lkt"], nth(b))
                cp(LK[:], PA[:, 0:SB * 32].rearrange("p (s c) -> p s c", c=32)).then_inc(sem["lk"], 1)
                dve.wait_ge(sem["st"], nth(b))
                for h in range(2):
                    rows = slice(GROUP * h, GROUP * h + GROUP)
                    last = nc.vector.scalar_tensor_tensor(
                        out=TMP[rows, :, :], in0=PD[rows, :].rearrange("p (s i) -> p s i", i=P)[:, :, rows],
                        scalar=1.0 / GROUP, in1=BIAS[rows, :].unsqueeze(1).to_broadcast([GROUP, SB, GROUP]),
                        op0=ALU.mult, op1=ALU.add)
                last.then_inc(sem["tb"], 1)
                dve.wait_ge(sem["tb"], nth(b))
                for h in range(2):
                    rows = slice(GROUP * h, GROUP * h + GROUP)
                    last = nc.vector.scalar_tensor_tensor(out=AT[rows, :, rows], in0=TMP[rows, :, :], scalar=0.0,
                                                          in1=TMP[rows, :, :], op0=ALU.max, op1=ALU.mult)
                last.then_inc(sem["att"], 1)
                dve.wait_ge(sem["bi"], nth(b))
                dve.sem_inc(sem["passed"], 1)
                for s in range(SB):
                    last = nc.vector.max(TOP8[:, s, :], BI[:, s, :])
                last.then_inc(sem["route"], 1)
                dve.wait_ge(sem["route"], nth(b * 9, 0))
                dve.sem_inc(sem["passed"], 1)
                for s in range(SB):
                    last = nc.vector.match_replace(out=CUT[:, s, :], in_to_replace=TOP8[:, s, :],
                                                   in_values=BI[:, s, :], imm_value=LOWEST)
                last.then_inc(sem["route"], 1)
                dve.wait_ge(sem["route"], nth(b * 9, 1))
                tt(CUT[:], CUT[:], BI[:], ALU.not_equal).then_inc(sem["route"], 1)
                dve.wait_ge(sem["route"], nth(b * 9, 2))
                tt(SIG[:], SIG[:], CUT[:], ALU.mult).then_inc(sem["route"], 1)
                dve.wait_ge(sem["route"], nth(b * 9, 3))
                nc.vector.tensor_reduce(WS[:, 0, :], SIG[:], AX.X, ALU.add).then_inc(sem["route"], 1)
                dve.wait_ge(sem["route"], nth(b * 9, 4))
                ts(WS[:, 1, :], WS[:, 0, :], 1e-8, None, ALU.add).then_inc(sem["route"], 1)
                dve.wait_ge(sem["route"], nth(b * 9, 5))
                nc.vector.reciprocal(WS[:, 2, :], WS[:, 1, :]).then_inc(sem["route"], 1)
                dve.wait_ge(sem["route"], nth(b * 9, 6))
                tt(BI[:], SIG[:], WS[:, 2, :].unsqueeze(2).to_broadcast([P, SB, E0]), ALU.mult).then_inc(sem["route"], 1)
                dve.wait_ge(sem["route"], nth(b * 9, 7))
                cp(CS[:, :, 0:E0], BI[:]).then_inc(sem["route"], 1)
                dve.wait_ge(sem["route"], nth(b * 9, 8))
                tt(CS[:, :, E0:2 * E0], BI[:], CS[:, :, 0:E0], ALU.subtract).then_inc(sem["cs"], 1)
                for h, (ot, g, pt) in enumerate((("ot0", "g0", PB), ("ot1", "g1", PC))):
                    dve.wait_ge(sem[ot], nth(b))
                    dve.wait_ge(sem[g], nth(b))
                    tt(OG[:, h, :], pt[:], G[:, h, :], ALU.mult).then_inc(sem[("og0", "og1")[h]], 1)
                    if more and h == 0:
                        x_stats(b + 1)
                        x_apply(b + 1)
                if more:
                    z_stats(b + 1)
                    z_apply(b + 1)
                else:
                    weights_low(0)
                dve.wait_ge(sem["yp"], nth(b))
                dve.wait_ge(sem["xr"], b + 1)
                tt(YT[:], PD[:].rearrange("p (s d) -> p s d", d=D), BOB[:].unsqueeze(1).to_broadcast([P, SB, D]),
                   ALU.add).then_inc(sem["y"], 1)
                dve.wait_ge(sem["y"], nth(b))
                norm_stats(dve, "y", lambda s: YT[:, s, :], b)
                if more:
                    turned_z(b + 1)
                norm_apply(dve, "y", lambda s: YT[:, s, :], lambda s: YT[:, s, :], "yn", b)
                if more:
                    low_z_and_bias(b + 1)
                if not more:
                    scale_shift_add(dve, b)

            dve.wait_ge(sem["x_in"], 16 * 1)
            x_stats(0)
            x_apply(0)
            z_stats(0)
            z_apply(0)
            dve.wait_ge(sem["c_in"], 16 * len(consts))
            cp(PICK64[:], STAGE[:, 0:64])
            cp(PICK8[:], STAGE[0:16, 64:72])
            cp(WZH[:], WZR[:]).then_inc(sem["wz_h"], 1)
            nc.vector.memset(AT[:], 0.0)
            dve.wait_ge(sem["wz_h"], nth())
            tt(WZL[:], WZR[:], WZH[:], ALU.subtract).then_inc(sem["wz_l"], 1)
            dve.wait_ge(sem["wz_l"], nth())
            turned_z(0)
            low_z_and_bias(0)
            dve.wait_ge(sem["x_rest"], 16 * (B - 1))
            with dve.Fori(0, B - 1) as b:
                batch(b, True)
            batch(B - 1, False)

            def low_half(n, q):
                u = q % UN0
                M = P if u < PAIRS else 64
                dve.wait_ge(sem["hi"], nth_free(n * UN0, q))
                dve.wait_ge(sem["down"], nth_free(n * UN0, q - 3))
                tt(HL[u % 3][0:M, :], HF[u % 3][0:M, :], HH[u % 3][0:M, :], ALU.subtract).then_inc(sem["lo"], 1)

            def add_experts(n):
                dve.wait_ge(sem["ytp"], nth(n))
                xs = X[:, bass.ds(n * 4, 4), :].rearrange("p s d -> p (s d)")
                tt(xs, xs, bank(6), ALU.add).then_inc(sem["d_x"], 1)

            def expert_tile(n, first):
                for p in range(UN0):
                    soon = p + 6
                    if first and soon % (PAIRS // WCH) == 0 and soon < PAIRS:
                        weights_low(soon // (PAIRS // WCH))
                    if p >= 2 or not first:
                        low_half(n, p - 2)
                    M = P if p < PAIRS else 64
                    dve.wait_ge(sem["silu"], nth_free(n * UN0, p))
                    dve.wait_ge(sem["lo"], nth_free(n * UN0, p - 3))
                    if p < PAIRS:
                        dve.wait_ge(sem["bc"], nth_free(n * PAIRS, p))
                        tt(HF[p % 3][:], SU[p % 2][:], bank(3 + p % 2), ALU.mult).then_inc(sem["hf"], 1)
                    else:
                        cp(HF[p % 3][0:M, :], SU[p % 2][0:M, :]).then_inc(sem["hf"], 1)
                    if p == TURN and not first:
                        add_experts(n - 1)

            expert_tile(0, True)
            with dve.Fori(0, NT - 1) as i:
                expert_tile(i + 1, False)
            low_half(NT, -2)
            low_half(NT, -1)
            add_experts(NT - 1)

            dve.wait_ge(sem["p_in"], 16 * 4)
            dve.wait_ge(sem["d_x"], nth_free(0, NT - 1))
            cp(WV1H[:], WV1[:]).then_inc(sem["wz_h"], 1)
            nc.vector.memset(LG[:, :, E1:16], LOWEST)
            nc.vector.memset(SEL2[:, :, 2:8], LOWEST)
            dve.wait_ge(sem["wz_h"], nth(0, 1))
            tt(WV1L[:], WV1[:], WV1H[:], ALU.subtract).then_inc(sem["wz_l"], 1)
            def e_stats(b):
                norm_stats(dve, "e", lambda s: x_sub(b, s), b)

            def e_apply(b):
                norm_apply(dve, "e", lambda s: x_sub(b, s), lambda s: XN1[:, s, :], "exn", b)

            def batch2(b, more):
                if more:
                    e_stats(b + 1)
                if more:
                    dve.wait_ge(sem["ext"], nth(b))
                    e_apply(b + 1)
                dve.wait_ge(sem["lg"], nth(b))
                tt(LG[:, :, 0:E1], PD[:, 0:SB * E1].rearrange("p (s e) -> p s e", e=E1),
                   GBB[:].unsqueeze(1).to_broadcast([P, SB, E1]), ALU.add).then_inc(sem["route2"], 1)
                dve.wait_ge(sem["route2"], nth(b * 10, 0))
                dve.sem_inc(sem["passed"], 1)
                for s in range(SB):
                    last = nc.vector.max(TOP2[:, s, :], LG[:, s, 0:14])
                last.then_inc(sem["route2"], 1)
                dve.wait_ge(sem["route2"], nth(b * 10, 1))
                cp(SEL2[:, :, 0:2], TOP2[:, :, 0:2]).then_inc(sem["route2"], 1)
                tt(SH[:], LG[:, :, 0:E1], TOP2[:, :, 0:1].to_broadcast([P, SB, E1]), ALU.subtract).then_inc(sem["shift"], 1)
                dve.wait_ge(sem["route2"], nth(b * 10, 2))
                dve.sem_inc(sem["passed"], 1)
                for s in range(SB):
                    last = nc.vector.match_replace(out=CUT2[:, s, 0:14], in_to_replace=SEL2[:, s, :],
                                                   in_values=LG[:, s, 0:14], imm_value=-LOWEST)
                last.then_inc(sem["route2"], 1)
                dve.wait_ge(sem["route2"], nth(b * 10, 3))
                tt(MASK2[:], CUT2[:, :, 0:E1], LG[:, :, 0:E1], ALU.not_equal).then_inc(sem["route2"], 1)
                dve.wait_ge(sem["route2"], nth(b * 10, 4))
                dve.wait_ge(sem["ex"], nth(b))
                tt(GM[:], EX[:], MASK2[:], ALU.mult).then_inc(sem["route2"], 1)
                dve.wait_ge(sem["route2"], nth(b * 10, 5))
                nc.vector.tensor_reduce(GSUM[:, 0, :], GM[:], AX.X, ALU.add).then_inc(sem["route2"], 1)
                dve.wait_ge(sem["route2"], nth(b * 10, 6))
                nc.vector.reciprocal(GSUM[:, 1, :], GSUM[:, 0, :]).then_inc(sem["route2"], 1)
                dve.wait_ge(sem["route2"], nth(b * 10, 7))
                tt(GATE[:], GM[:], GSUM[:, 1, :].unsqueeze(2).to_broadcast([P, SB, E1]), ALU.mult).then_inc(sem["route2"], 1)
                dve.wait_ge(sem["route2"], nth(b * 10, 8))
                cp(GS[:, bass.ds(b * SB, SB), 0:E1], GATE[:]).then_inc(sem["route2"], 1)
                dve.wait_ge(sem["route2"], nth(b * 10, 9))
                tt(GS[:, bass.ds(b * SB, SB), E1:2 * E1], GATE[:], GS[:, bass.ds(b * SB, SB), 0:E1],
                   ALU.subtract).then_inc(sem["gs"], 1)
                dve.wait_ge(sem["vp"], nth(b))
                for g in range(HG):
                    x = 32 * g
                    last = tt(V1[:, bass.ds(b * HG + g, 1), :, :, :].rearrange("p g s j d -> p (g s) (j d)"),
                              PC[:].rearrange("p (s e) -> p s e", e=D)[:, :, x:x + 32],
                              BVB1[:, x:x + 32].unsqueeze(1).to_broadcast([P, SB, 32]), ALU.add)
                last.then_inc(sem["ve"], 1)
                dve.wait_ge(sem["pp"], nth(b))
                dve.wait_ge(sem["ph_w"], b * 32 + 16)
                ts(PF[:].rearrange("p (c i) -> p i c", i=NI), PB[:].rearrange("p (i c) -> p i c", i=NI),
                   COL1[:, 0:1], None, ALU.add).then_inc(sem["pf"], 1)
                dve.wait_ge(sem["ph"], nth(b))
                tt(PL[:], PF[:], PH[:], ALU.subtract).then_inc(sem["pl"], 1)

            e_stats(0)
            e_apply(0)
            with dve.Fori(0, B - 1) as b:
                batch2(b, True)
            batch2(B - 1, False)

            def slot(x, idx, g, par):
                mb = slot_bank(idx)
                kind, u, ahead = seq_of(idx)
                gp = (par + ahead) % 2
                dve.wait_ge(sem["mx"], nth_free(x))
                if kind == "max":
                    half, c4, j, h = u // 32, (u % 32) // 8, (u % 8) // 2, u % 2
                    nc.vector.tensor_reduce(MX[gp][:, half, j, c4, h:h + 1], mb, AX.X, ALU.max).then_inc(sem["red"], 1)
                    if u % 32 == 31:
                        dve.wait_ge(sem["red"], nth_free(x))
                        nc.vector.tensor_reduce(MN[gp][:, half, :], MX[gp][:, half, :, :, :].rearrange("p j c h -> p (j c) h"),
                                                AX.X, ALU.max, negate=True).then_inc(sem["neg"], 1)
                else:
                    e = (g + ahead) * 2 + u
                    dve.wait_ge(sem["m_w"], e * 32 + 32)
                    cp(MH[u][:], mb[0:HG * 4, 0:P]).then_inc(sem["mhi"], 1)
                    dve.wait_ge(sem["mhi"], nth(e))
                    tt(ML[u][:], mb[0:HG * 4, 0:P], MH[u][:], ALU.subtract).then_inc(sem["red"], 1)

            for idx in range(PRO):
                slot(idx, (idx, "pro"), 0, 0)
            with dve.Fori(0, NG // 2 - 1) as i:
                for par in range(2):
                    for idx in range(SLOTS):
                        slot((i * 2 + par) * SLOTS + (PRO + idx), (idx, "body"), i * 2 + par, par)
            for idx in range(SLOTS):
                slot((NG - 2) * SLOTS + PRO + idx, (idx, "body"), NG - 2, 0)
            for idx in range(SLOTS_END):
                slot((NG - 1) * SLOTS + PRO + idx, (idx, "end"), NG - 1, 1)

            def low_half(n, q):
                u = q % U1
                dve.wait_ge(sem["hi1"], nth_free(n * U1, q))
                dve.wait_ge(sem["dn1"], nth_free(n * U1, q - 4))
                tt(HL1[u % 4][:], HF1[u % 2][:], HH1[u % 4][:], ALU.subtract).then_inc(sem["lo1"], 1)

            def finish(n):
                dve.wait_ge(sem["ytp2"], nth(n))
                dve.wait_ge(sem["out_s"], n * 16 + 16)
                tt(FIN[:].rearrange("p s d -> p (s d)"), X[:, bass.ds(n * 4, 4), :].rearrange("p s d -> p (s d)"),
                   bank(6), ALU.add).then_inc(sem["fin"], 1)

            def expert_tile(n, first):
                u0 = n * U1
                for p in range(U1):
                    dve.wait_ge(sem["s1"], nth_free(u0, p))
                    dve.wait_ge(sem["hf1"], nth_free(u0, before(p, 2, U1)))
                    dve.wait_ge(sem["h0"], nth_free(u0, p))
                    nc.vector.scalar_tensor_tensor(
                        out=AH[p % 2][:], in0=bank(2 + p % 2), scalar=COL1[:, 2 + p:3 + p], in1=S1[p % 2][:],
                        op0=ALU.add, op1=ALU.mult).then_inc(sem["ah"], 1)
                    dve.wait_ge(sem["ah"], nth_free(u0, p))
                    dve.wait_ge(sem["bg"], nth_free(n * E1, p // 2))
                    dve.wait_ge(sem["lo1"], nth_free(u0, before(p, 2, U1)))
                    tt(HF1[p % 2][:], AH[p % 2][:], bank((4, 7)[p // 2 % 2]), ALU.mult).then_inc(sem["hf1"], 1)
                    if p >= 1 or not first:
                        low_half(n, p - 1)
                    if p == 1:
                        dve.wait_ge(sem["den_in"], n * 16 + 16)
                        dve.wait_ge(sem["rd_w"], n * 16 + 16)
                        nc.vector.reciprocal(RD[:], DEN[:]).then_inc(sem["rec"], 1)
                    if p == TURN1 and not first:
                        finish(n - 1)

            expert_tile(0, True)
            with dve.Fori(0, NT - 1) as i:
                expert_tile(i + 1, False)
            low_half(NT, -1)
            finish(NT - 1)

        @block.scalar
        def _(act):
            for name in ("silu", "hi", "exq", "osb", "s1", "hi1", "yt", "y2s"):
                act.sem_inc(sem[name], CREDIT)
            fn, copy = nc.scalar.activation, ACT.Copy

            def std(pre, b):
                act.wait_ge(sem[pre + "_var"], nth(b))
                fn(SD[:], VE[:], ACT.Sqrt).then_inc(sem[pre + "_std"], 1)

            def turned_x(b):
                act.wait_ge(sem["xt"], nth(b))
                act.wait_ge(sem["xtl"], b + 1)
                fn(XF[:], PA[:], copy).then_inc(sem["xf"], 1)

            def high_z(b):
                act.wait_ge(sem["zf"], nth(b))
                fn(ZTH[:], ZF[:], copy).then_inc(sem["zth"], 1)

            def weights_high():
                act.wait_ge(sem["ot1"], nth(0, B - 1))
                act.wait_ge(sem["xtl"], B + 1)
                act.wait_ge(sem["w_in"], 16 * 3)
                for c in range(WCH):
                    fn(WUH[:, wu_cols(c)], WUL_RAW[:, wu_cols(c)], copy).then_inc(sem["wu_h"], 1)
                    fn(WDH[:, wd_units(c), :], WDL_RAW[:, wd_units(c), :], copy).then_inc(sem["wd_h"], 1)
                fn(WDH[0:64, PAIRS, :], WDL_RAW[0:64, PAIRS, :], copy).then_inc(sem["wd_h"], 1)

            def batch(b, more):
                act.wait_ge(sem["aff"], nth(b))
                fn(SIG[:].rearrange("p s e -> p (s e)"), PC[:, 0:SB * E0], ACT.Sigmoid).then_inc(sem["sig"], 1)
                act.wait_ge(sem["qp"], nth(b))
                fn(QA[:], PB[:], ACT.Silu, bias=COLS[:, 2:3]).then_inc(sem["qa"], 1)
                act.wait_ge(sem["qs"], nth(b))
                fn(QB[:], PC[:], ACT.Silu, bias=COLS[:, 3:4]).then_inc(sem["qb"], 1)
                act.wait_ge(sem["vb1"], nth(b))
                fn(V[:, 0:4, :], V[:, 0:4, :], ACT.Silu).then_inc(sem["v1"], 1)
                act.wait_ge(sem["vb2"], nth(b))
                fn(V[:, 4:8, :], V[:, 4:8, :], ACT.Silu).then_inc(sem["v2"], 1)
                act.wait_ge(sem["g0p"], nth(b))
                fn(G[:, 0, :], PB[:], ACT.Silu, bias=COLS[:, 8:9]).then_inc(sem["g0"], 1)
                act.wait_ge(sem["g1p"], nth(b))
                fn(G[:, 1, :], PC[:], ACT.Silu, bias=COLS[:, 9:10]).then_inc(sem["g1"], 1)
                act.wait_ge(sem["kvp"], nth(b))
                fn(KV[32:64, :], PA[32:64, TB:TB + HV], copy, scale=1.0 / N).then_inc(sem["kv"], 1)
                if more:
                    std("x", b + 1)
                act.wait_ge(sem["cst"], nth(b))
                fn(CWT[:, bass.ds(b * N, N)], PD[:], copy).then_inc(sem["cwt"], 1)
                if more:
                    std("z", b + 1)
                    turned_x(b + 1)
                if not more:
                    weights_high()
                std("y", b)
                if more:
                    high_z(b + 1)

            std("x", 0)
            std("z", 0)
            act.wait_ge(sem["c_in"], 16 * len(consts))
            turned_x(0)
            high_z(0)
            with act.Fori(0, B - 1) as b:
                batch(b, True)
            batch(B - 1, False)

            def high_half(n, q):
                u = q % UN0
                M = P if u < PAIRS else 64
                act.wait_ge(sem["hf"], nth_free(n * UN0, q))
                act.wait_ge(sem["down"], nth_free(n * UN0, q - 3))
                fn(HH[u % 3][0:M, :], HF[u % 3][0:M, :], copy).then_inc(sem["hi"], 1)

            def sums_out(n):
                act.wait_ge(sem["down"], nth_free(n * UN0, UN0 - 1))
                fn(YF[:], bank(5), copy).then_inc(sem["yt"], 1)

            def expert_tile(n, first):
                for p in range(UN0):
                    M = P if p < PAIRS else 64
                    if p == LAG and not first:
                        sums_out(n - 1)
                    act.wait_ge(sem["up"], nth_free(n * UN0, p))
                    act.wait_ge(sem["hf"], nth_free(n * UN0, before(p, 2, UN0)))
                    fn(SU[p % 2][0:M, :], bank(p % 3)[0:M, :], ACT.Silu).then_inc(sem["silu"], 1)
                    if p >= 1 or not first:
                        high_half(n, p - 1)

            expert_tile(0, True)
            with act.Fori(0, NT - 1) as i:
                expert_tile(i + 1, False)
            high_half(NT, -1)
            sums_out(NT - 1)

            def batch2(b, more):
                act.wait_ge(sem["ext"], nth(b))
                act.wait_ge(sem["extl"], b + 1)
                fn(XF1[:], PA[:], copy).then_inc(sem["exf"], 1)
                fn(XFP[:].rearrange("p (c i) -> p c i", i=NI), PA[:].rearrange("p (i c) -> p c i", i=NI),
                   copy).then_inc(sem["xfp"], 1)
                if more:
                    std("e", b + 1)
                act.wait_ge(sem["shift"], nth(b))
                fn(EX[:], SH[:], ACT.Exp).then_inc(sem["ex"], 1)
                act.wait_ge(sem["pf"], nth(b))
                fn(PH[:], PF[:], copy).then_inc(sem["ph"], 1)

            std("e", 0)
            with act.Fori(0, B - 1) as b:
                batch2(b, True)
            batch2(B - 1, False)
            act.wait_ge(sem["gstp"], nth())
            for k, t in ((2, PC), (3, PD), (0, PA), (1, PB)):
                fn(GTT[:, N * k:N * k + N], t[0:2 * E1, :], copy).then_inc(sem["gt"], 1)

            def exps(s, k):
                for pair in range(2):
                    act.wait_ge(sem["sc"], nth_free(s * 2, 2 * k + pair))
                    act.wait_ge(sem["av"], s + (k - 1 + AV0))
                    fn(EX1[(2 * k + pair) % 4][:], (PA, PB)[pair][:], ACT.Exp, scale=SCALE).then_inc(sem["exq"], 1)

            def out_half(g, k):
                act.wait_ge(sem["av"], g * 16 + (k + 1 + AV0))
                act.wait_ge(sem[OD_W[k // 8]], g * 16 + 16)
                fn(OSB[k // 8][:], bank(7), copy).then_inc(sem["osb"], 1)

            act.wait_ge(sem["lr"], 16 * (2 * HG + 15))
            exps(0, 0)
            with act.Fori(0, NG // 2 - 1) as i:
                for par in range(2):
                    for k in range(16):
                        exps((i * 2 + par) * 16, k + 1)
                        if k % 8 == 7:
                            out_half(i * 2 + par, k)
            for g in range(NG - 2, NG):
                for k in range(16):
                    if k < 15 or g < NG - 1:
                        exps(g * 16, k + 1)
                    if k % 8 == 7:
                        out_half(g, k)

            def high_half(n, q):
                u = q % U1
                act.wait_ge(sem["hf1"], nth_free(n * U1, q))
                act.wait_ge(sem["dn1"], nth_free(n * U1, q - 4))
                fn(HH1[u % 4][:], HF1[u % 2][:], copy).then_inc(sem["hi1"], 1)

            def sums_out(n):
                act.wait_ge(sem["dn1"], nth_free(n * U1, U1 - 1))
                fn(Y2[:], bank(5), ACT.Identity, bias=COL1[:, 1:2]).then_inc(sem["y2s"], 1)

            def expert_tile(n, first):
                u0 = n * U1
                for p in range(U1):
                    if p == LAG1 and not first:
                        sums_out(n - 1)
                    act.wait_ge(sem["h1"], nth_free(u0, p))
                    act.wait_ge(sem["ah"], nth_free(u0, before(p, 2, U1)))
                    fn(S1[p % 2][:], bank(p % 2), ACT.Silu, bias=COL1[:, 2 + U1 + p:3 + U1 + p]).then_inc(sem["s1"], 1)
                    if p >= 1 or not first:
                        high_half(n, p - 1)

            expert_tile(0, True)
            with act.Fori(0, NT - 1) as i:
                expert_tile(i + 1, False)
            high_half(NT, -1)
            sums_out(NT - 1)

        @block.tensor
        def _(pe):
            for name in ("up", "bc", "down", "sc", "mx", "h1", "h0", "bg", "dn1"):
                pe.sem_inc(sem[name], CREDIT)
            pe.sem_inc(sem["av"], AV0)
            pe.sem_inc(sem["pj"], 1)
            mm, tr = nc.tensor.matmul, nc.tensor.transpose
            pe.wait_ge(sem["wz_l"], nth())

            def head(b):
                pe.wait_ge(sem["xn"], nth(b))
                for s in range(SB):
                    last = tr(PA[:, P * s:P * s + P], XN[:, s, :], IDN[:])
                last.then_inc(sem["xt"], 1)
                pe.wait_ge(sem["z"], nth(b))
                for s in range(SB):
                    last = tr(PB[:, P * s:P * s + P], Z[:, s, :], IDN[:])
                last.then_inc(sem["zt"], 1)
                pe.wait_ge(sem["xf"], nth(b))
                for s in range(SB):
                    last = mm(PC[:, E0 * s:E0 * s + E0], XF[:, P * s:P * s + P], CEN[:], start=True, stop=True)
                last.then_inc(sem["aff"], 1)

            def batch(b):
                pe.wait_ge(sem["zth"], nth(b))
                pe.wait_ge(sem["ztl"], nth(b))

                def project(dst, c0, done):
                    for h in range(2):
                        c = slice(TB * h, TB * h + TB)
                        last = mm3(dst[:, c], (WZH[:, c0:c0 + P], WZL[:, c0:c0 + P]), (ZTH[:, c], ZTL[:, c]), True, True)
                    last.then_inc(sem[done], 1)

                def values(dst, s0, done):
                    c = slice(2 * P, 2 * P + HV)
                    for s in range(4):
                        t = slice(P * (s0 + s), P * (s0 + s) + P)
                        last = mm3(dst[:, HV * s:HV * s + HV], (ZTH[:, t], ZTL[:, t]), (WZH[:, c], WZL[:, c]), True, True)
                    last.then_inc(sem[done], 1)

                project(PB, 0, "qp")
                pe.wait_ge(sem["bi"], nth(b))
                pe.wait_ge(sem["sig"], nth(b))
                project(PC, P, "qs")
                values(PD, 0, "v1p")
                values(PA, 4, "v2p")
                pe.wait_ge(sem["qa"], nth(b))
                project(PB, 2 * P + HV, "g0p")
                pe.wait_ge(sem["qb"], nth(b))
                project(PC, 3 * P + HV, "g1p")
                pe.wait_ge(sem["c_in"], 16 * len(consts))
                pe.wait_ge(sem["qr"], nth(b))
                pe.wait_ge(sem["vb2"], nth(b))
                for s in range(SB):
                    last = tr(PA[:, 32 * s:32 * s + 32], QA[96:128, P * s:P * s + P], IDN[96:128, 96:128])
                last.then_inc(sem["lkt"], 1)
                pe.wait_ge(sem["vb1"], nth(b))
                pe.wait_ge(sem["qqd"], b * 16 + 16)
                for s in range(SB):
                    t = slice(P * s, P * s + P)
                    last = mm(PD[:, t], QA[64:96, t], QQ[64:96, t], start=True, stop=True)
                last.then_inc(sem["st"], 1)
                pe.wait_ge(sem["lk"], nth(b))
                pe.wait_ge(sem["v1"], nth(b))
                pe.wait_ge(sem["v2"], nth(b))
                for s in range(SB):
                    last = mm(PA[32:64, TB:TB + HV], LK[:, s, :], V[:, s, :], start=(s == 0), stop=(s == SB - 1))
                last.then_inc(sem["kvp"], 1)
                pe.wait_ge(sem["kv"], nth(b))
                pe.wait_ge(sem["att"], nth(b))
                for h, (pt, g, done) in enumerate(((PB, "g0", "ot0"), (PC, "g1", "ot1"))):
                    pe.wait_ge(sem[g], nth(b))
                    rows = slice(P * h, P * h + P)
                    for q in range(2):
                        o = pt[:, TB * q:TB * q + TB]
                        mm(o, KV[32:64, rows], QA[32:64, TB * q:TB * q + TB], start=True, stop=False)
                        for s in range(4):
                            last = mm(o[:, P * s:P * s + P], V[:, 4 * q + s, rows], AT[:, 4 * q + s, :],
                                      start=False, stop=(s == 3))
                    last.then_inc(sem[done], 1)
                pe.wait_ge(sem["cs"], nth(b))
                for s in range(SB):
                    last = tr(PD[:, P * s:P * s + P], CS[:, s, :].bitcast(F32), IDN[:])
                last.then_inc(sem["cst"], 1)
                pe.wait_ge(sem["cwt"], nth(b))
                pe.wait_ge(sem["og0"], nth(b))
                pe.wait_ge(sem["og1"], nth(b))
                for s in range(SB):
                    for h in range(H1):
                        last = mm(PD[:, P * s:P * s + P], OG[:, h, P * s:P * s + P], WO0[:, h, :],
                                  start=(h == 0), stop=(h == H1 - 1))
                last.then_inc(sem["yp"], 1)

            head(0)
            with pe.Fori(0, B - 1) as b:
                batch(b)
                head(b + 1)
            batch(B - 1)

            pe.wait_ge(sem["xtl"], B + 1)
            pe.wait_ge(sem["cwt"], nth(0, B - 1))

            def project_down(n, q):
                u = q % UN0
                M = P if u < PAIRS else 64
                pe.wait_ge(sem["lo"], nth_free(n * UN0, q))
                if u == 0:
                    pe.wait_ge(sem["yt"], nth_free(n, -1))
                mm3(bank(5), (WDH[0:M, u, :], WDL[0:M, u, :]), (HH[u % 3][0:M, :], HL[u % 3][0:M, :]),
                    u == 0, u == UN0 - 1).then_inc(sem["down"], 1)

            def turn_out(n):
                pe.wait_ge(sem["yt"], nth_free(n))
                pe.wait_ge(sem["d_x"], nth_free(n, -1))
                for s in range(4):
                    last = tr(bank(6)[:, P * s:P * s + P], YF[:, P * s:P * s + P], IDN[:])
                last.then_inc(sem["ytp"], 1)

            def expert_tile(n, first):
                tok = bass.ds(n * TB, TB)
                xh, xl = XTH[:, tok], XTL[:, tok]
                for p in range(UN0):
                    M = P if p < PAIRS else 64
                    if first and p % (PAIRS // WCH) == 0 and p < PAIRS:
                        pe.wait_ge(sem["wu_l"], nth(0, p // (PAIRS // WCH)))
                        pe.wait_ge(sem["pickw"], nth(0, p // (PAIRS // WCH)))
                    if M < P:
                        pe.wait_ge(sem["c_in"], 16 * len(consts))
                    pe.wait_ge(sem["silu"], nth_free(n * UN0, p - 3))
                    c = slice(P * p, P * p + M)
                    mm3(bank(p % 3)[0:M, :], (WUH[:, c], WUL[:, c]), (xh, xl), True, True).then_inc(sem["up"], 1)
                    if p < PAIRS:
                        pe.wait_ge(sem["hf"], nth_free(n * UN0, p - 2 if p >= 2 else p - 3))
                        mm(bank(3 + p % 2), PICKW[:, 2 * p:2 * p + 2, :].rearrange("p e f -> p (e f)"),
                           CWT[:, tok], start=True, stop=True).then_inc(sem["bc"], 1)
                    if first and p >= LAG and (p - LAG) % (PAIRS // WCH) == 0:
                        pe.wait_ge(sem["wd_l"], nth(0, (p - LAG) // (PAIRS // WCH)))
                    if p >= LAG or not first:
                        project_down(n, p - LAG)
                    if p == TURN and not first:
                        turn_out(n - 1)

            expert_tile(0, True)
            pe.wait_ge(sem["wd_l"], nth(0, WCH))
            with pe.Fori(0, NT - 1) as i:
                expert_tile(i + 1, False)
            for q in range(-LAG, 0):
                project_down(NT, q)
            turn_out(NT - 1)

            pe.wait_ge(sem["d_x"], nth_free(0, NT - 1))
            pe.wait_ge(sem["wz_l"], nth(0, 1))
            with pe.Fori(0, B) as b:
                pe.wait_ge(sem["exn"], nth(b))
                for s in range(SB):
                    last = tr(PA[:, P * s:P * s + P], XN1[:, s, :], IDN[:])
                last.then_inc(sem["ext"], 1)
                pe.wait_ge(sem["exf"], nth(b))
                for s in range(SB):
                    last = mm(PD[:, E1 * s:E1 * s + E1], XF1[:, P * s:P * s + P], GW[:], start=True, stop=True)
                last.then_inc(sem["lg"], 1)
                pe.wait_ge(sem["xfp"], nth(b))
                for s in range(SB):
                    last = mm(PC[:, P * s:P * s + P], XFP[:, P * s:P * s + P], WV1[:], start=True, stop=True)
                last.then_inc(sem["vp"], 1)
                pe.wait_ge(sem["extl"], b + 2)
                for h in range(2):
                    t = bass.ds(b * N + TB * h, TB)
                    last = mm3(PB[:, TB * h:TB * h + TB], (WV1H[:], WV1L[:]), (XTH[:, t], XTL[:, t]), True, True)
                last.then_inc(sem["pp"], 1)

            pe.wait_ge(sem["gs"], nth(0, B - 1))
            pe.wait_ge(sem["ve"], nth(0, B - 1))
            pe.wait_ge(sem["pf"], nth(0, B - 1))
            for s in range(SUB):
                last = tr((PA, PB, PC, PD)[s // SB][0:2 * E1, P * (s % SB):P * (s % SB) + P], GS[:, s, :].bitcast(F32), IDN[:])
            last.then_inc(sem["gstp"], 1)
            pe.wait_ge(sem["gt"], nth(0, 1))

            def scores(g, k, par, pair):
                half, kc = k // 8, k % 8
                if kc == 0 and pair == 0:
                    pe.wait_ge(sem["m_r"], g * 32 + 16 * (half + 1))
                pe.wait_ge(sem["exq"], nth_free(g * 32, 2 * (k - 1) + pair))
                for jj in range(2):
                    last = mm((PA, PB)[pair][:, TB * jj:TB * jj + TB], L[par][0:MR + 2 * HG, 2 * pair + jj, P * kc:P * kc + P],
                              R[par][0:MR + 2 * HG, TB * half:TB * half + TB], start=True, stop=True)
                last.then_inc(sem["sc"], 1)

            def products(g, k, par):
                half, kc = k // 8, k % 8
                if k == 0:
                    pe.wait_ge(sem["va"], nth(g))
                pe.wait_ge(sem["exq"], nth_free(g * 32, 2 * k + 1))
                if kc == 0:
                    pe.wait_ge(sem["osb"], nth_free(g * 2, half - 1))
                for j in range(HG):
                    last = mm(bank(7)[32 * j:32 * j + 32, :], VA[par][:, kc, j, :],
                              EX1[(2 * k + j // 2) % 4][:, TB * (j % 2):TB * (j % 2) + TB], start=(kc == 0), stop=(kc == 7))
                last.then_inc(sem["av"], 1)

            def pslot(x, idx, g, par):
                kind, u, ahead = seq_of(idx)
                gp = (par + ahead) % 2
                mb = slot_bank(idx)
                if not (idx[1] == "pro" and idx[0] < 3):
                    pe.wait_ge(sem["red"], nth_free(x, -3))
                if kind == "max":
                    if u == 0:
                        pe.wait_ge(sem["lr"], (g + ahead) * (15 * 16) + 16 * (2 * HG + 15))
                    c, j, h = u // 8, (u % 8) // 2, u % 2
                    mm(mb, L[gp][0:MR, j, P * c:P * c + P], R[gp][0:MR, TB * h:TB * h + TB],
                       start=True, stop=True).then_inc(sem["mx"], 1)
                else:
                    pe.wait_ge(sem["neg"], nth((g + ahead) * 2 + u))
                    tr(mb[0:HG * 4, 0:P], MN[gp][:, u, :], IDN[:]).then_inc(sem["mx"], 1)

            def group(g, par, kind):
                n_slots = SLOTS if kind == "body" else SLOTS_END
                for k in range(16):
                    mine = range(min(SLOTS * k // 16, n_slots), min(SLOTS * (k + 1) // 16, n_slots))
                    cuts = [mine[0:1], mine[1:2], mine[2:-1], mine[max(2, len(mine) - 1):]]
                    for part in range(4):
                        for idx in cuts[part]:
                            pslot(g * SLOTS + (PRO + idx), (idx, kind), g, par)
                        if part == 2:
                            products(g, k, par)
                        elif part < 2 and k < 15:
                            scores(g, k + 1, par, part)
                        elif part < 2 and kind == "body":
                            scores(g + 1, 0, 1 - par, part)

            pe.wait_ge(sem["ve"], nth(0, B - 1))
            for idx in range(PRO):
                pslot(idx, (idx, "pro"), 0, 0)
            pe.wait_ge(sem["gt"], nth(0, 3))
            for pair in range(2):
                scores(0, 0, 0, pair)
            with pe.Fori(0, NG // 2 - 1) as i:
                for par in range(2):
                    group(i * 2 + par, par, "body")
            group(NG - 2, 0, "body")
            group(NG - 1, 1, "end")

            pe.wait_ge(sem["w1_l"], nth(0, 2))
            pe.wait_ge(sem["osb"], nth_free(2 * NG - 1))

            def project_down(n, q):
                u = q % U1
                pe.wait_ge(sem["lo1"], nth_free(n * U1, q))
                if q == 0:
                    pe.wait_ge(sem["y2s"], nth_free(n, -1))
                    pe.sem_inc(sem["passed"], 1)
                    gates = GTT[:, bass.ds(n * TB, TB)]
                    mm(bank(5), B2H[:], gates, start=True, stop=False)
                    mm(bank(5), B2L[:], gates, start=False, stop=False)
                if q == PROJECT_AT:
                    pe.wait_ge(sem["on"], nth(n, 1))
                    mm(bank(5), WO1[:], ON[:], start=False, stop=False).then_inc(sem["pj"], 1)
                mm3(bank(5), (W2H[:, u, :], W2L[:, u, :]), (HH1[u % 4][:], HL1[u % 4][:]),
                    False, u == U1 - 1).then_inc(sem["dn1"], 1)

            def turn_out(n):
                pe.wait_ge(sem["y2s"], nth_free(n))
                pe.wait_ge(sem["fin"], nth_free(n, -1))
                for s in range(4):
                    last = tr(bank(6)[:, P * s:P * s + P], Y2[:, P * s:P * s + P], IDN[:])
                last.then_inc(sem["ytp2"], 1)

            def expert_tile(n, first):
                u0 = n * U1
                tok = bass.ds(n * TB, TB)
                xh, xl = XTH[:, tok], XTL[:, tok]
                for p in range(U1):
                    c = slice(P * p, P * p + P)
                    pe.wait_ge(sem["s1"], nth_free(u0, before(p, 2, U1)))
                    mm3(bank(p % 2), (W1H[:, 0, c], W1L[:, 0, c]), (xh, xl), True, True).then_inc(sem["h1"], 1)
                    pe.wait_ge(sem["ah"], nth_free(u0, before(p, 2, U1)))
                    mm3(bank(2 + p % 2), (W1H[:, 1, c], W1L[:, 1, c]), (xh, xl), True, True).then_inc(sem["h0"], 1)
                    if p % 2 == 0:
                        e = p // 2
                        pe.wait_ge(sem["c_in"], 16 * len(consts))
                        pe.wait_ge(sem["hf1"], nth_free(u0, 2 * e - 3))
                        mm(bank((4, 7)[e % 2]), PICK8[:, e:e + 1].to_broadcast([2 * E1, P]), GTT[:, tok],
                           start=True, stop=True).then_inc(sem["bg"], 1)
                    if p >= LAG1 or not first:
                        project_down(n, p - LAG1)
                    if p == TURN1 and not first:
                        turn_out(n - 1)

            expert_tile(0, True)
            with pe.Fori(0, NT - 1) as i:
                expert_tile(i + 1, False)
            for q in range(-LAG1, 0):
                project_down(NT, q)
            turn_out(NT - 1)


def kernel(**inputs):
    from concourse import bacc as _bacc
    from concourse.bass_utils import run_bass_kernel_spmd as _run

    f = {k: np.ascontiguousarray(v) for k, v in inputs.items()}
    x = f["L0_attn_x"]
    B, N, D = x.shape
    QK, E0, E1 = f["L0_attn_Wqk"].shape[0], f["L0_ffn_W_up"].shape[0], f["L1_ffn_w0"].shape[0]
    H1 = f["L1_ffn_w0"].shape[1]
    heads = f["L0_attn_gamma"].shape[0]
    swap = np.r_[QK // 2:QK, 0:QK // 2]
    wqk, bqk = f["L0_attn_Wqk"], f["L0_attn_bqk"]
    gam, bet = f["L0_attn_gamma"], f["L0_attn_beta"]

    def four(m):
        return np.concatenate([m] * heads, 0)

    bg = f["L0_attn_bg"].reshape(2, P)
    zero = np.zeros(P, np.float32)
    at = np.arange(P) % 64
    distance = np.clip(np.abs(at[:, None] - at[None, :64]), 0, 32)
    cols0 = np.stack([f["L0_attn_ln1_w"], f["L0_attn_ln1_b"], four(bqk), four(bqk[swap]), gam.reshape(-1),
                      bet.reshape(-1), gam[:, swap].reshape(-1), bet[:, swap].reshape(-1), bg[0], bg[1]]
                     + [zero] * 6, 1)
    halves0 = f["L1_ffn_b0"].reshape(-1, P)
    halves1 = f["L1_ffn_b1"].reshape(-1, P)
    cols1 = np.concatenate([f["L1_attn_bv"][:, None], f["L1_attn_bo"][:, None], halves0.T, halves1.T], 1)
    data = {
        "x": x,
        "wz": np.concatenate([four(wqk).T, four(wqk[swap]).T, f["L0_attn_Wv"].T, f["L0_attn_Wg"].T], 1),
        "cols0": cols0, "cols1": cols1,
        "bv0": f["L0_attn_bv"][None], "bo0": f["L0_attn_bo"][None], "wo0": f["L0_attn_Wo"].T,
        "ln2_w": f["L0_attn_ln2_w"][None], "ln2_b": f["L0_attn_ln2_b"][None], "bias": f["L0_attn_pos_emb"][distance],
        "centroids": f["L0_ffn_centroids"].T, "expert_biases": f["L0_ffn_expert_biases"][None],
        "w_up": np.concatenate([f["L0_ffn_W_up"].transpose(1, 0, 2).reshape(D, -1), f["L0_ffn_Ws_up"]], 1),
        "w_down": f["L0_ffn_W_down"].reshape(-1, D), "ws_down": f["L0_ffn_Ws_down"],
        "wv1": f["L1_attn_Wv"].T, "bv1": f["L1_attn_bv"][None], "wo1": f["L1_attn_Wo"].T,
        "gate_w": f["L1_ffn_gate_w"].T, "gate_b": f["L1_ffn_gate_b"][None],
        "w0": f["L1_ffn_w0"].transpose(2, 0, 1).reshape(D, -1), "w1": f["L1_ffn_w1"].transpose(2, 0, 1).reshape(D, -1),
        "w2": f["L1_ffn_w2"].transpose(0, 2, 1).reshape(E1 * H1, D),
        "b2": np.concatenate([f["L1_ffn_b2"]] * 2, 0),
    }
    data.update(shape_constants(N, QK))
    nc = _bacc.Bacc("TRN2", target_bir_lowering=False, num_devices=1)
    arrays, a = {}, {}
    for name, v in data.items():
        arrays["in_" + name] = np.ascontiguousarray(v)
        a[name] = nc.dram_tensor("in_" + name, v.shape, mybir.dt.from_np(v.dtype), kind="ExternalInput").ap()
    out = nc.dram_tensor("out_x", (B * N, D), F32, kind="ExternalOutput").ap()
    build_program(nc, a, out)
    r = _run(nc, [arrays], core_ids=[0])
    return r.results[0]["out_x"].reshape(B, N, D)
```
